# Optimizing a Trainium2 kernel written in Bass

```python
import numpy as np
import jax
import jax.numpy as jnp

def _softmax(x, axis=-1):
    return jax.nn.softmax(x, axis=axis)

def _gelu(x):
    return jax.nn.gelu(x, approximate=True)

def _silu(x):
    return jax.nn.silu(x)

def _sigmoid(x):
    return jax.nn.sigmoid(x)

def _layernorm(x, axis=-1, eps=1e-05):
    m = jnp.mean(x, axis=axis, keepdims=True)
    v = jnp.var(x, axis=axis, keepdims=True)
    return (x - m) / jnp.sqrt(v + eps)

def _scatter_add(tgt, idx, src, axis=0):
    return tgt.at[idx].add(src)

def _segment_sum(src, seg, n):
    return jax.ops.segment_sum(src, seg, n)
kernel_name = 'mk_perceiver_d1_seqx_r4_4c530e'

def setup_inputs(seed: int=0):
    np.random.seed(seed)
    _w = jnp.asarray

    def _rec_inputs():
        import jax
        import jax.numpy as jnp
        _rk = jax.random.key(seed)
        x = -0.0005207 + 1.001 * jax.random.normal(jax.random.fold_in(_rk, 1), (32, 32, 256), jnp.float32)
        _lenS = 32 - jax.random.randint(jax.random.fold_in(_rk, 7), (32,), 0, max(1, 32 // 4) + 1, jnp.int32)
        _lenS2 = 257 - jax.random.randint(jax.random.fold_in(_rk, 8), (32,), 0, max(1, 257 // 4) + 1, jnp.int32)
        _ctx_1024P = jax.random.normal(jax.random.fold_in(_rk, 11), (32, 16, 256), jnp.float32)
        _ctx_1024c = jax.random.dirichlet(jax.random.fold_in(_rk, 511), 0.3 * jnp.ones((16,), jnp.float32), (32, 257))
        _ctx_1024t = jnp.einsum('bsk,bkd->bsd', _ctx_1024c, _ctx_1024P)
        _ctx_1024t = _ctx_1024t * jax.lax.rsqrt(jnp.mean(jnp.square(_ctx_1024t)) + 1e-12) * 0.953939
        ctx_1024 = -5.72187e-05 + 0.999849 * (_ctx_1024t + 0.3 * jax.random.normal(jax.random.fold_in(_rk, 611), (32, 257, 256), jnp.float32))
        return (x, ctx_1024)
    x, ctx_1024 = _rec_inputs()

    def _L0_xattn_setup():
        import jax, jax.numpy as jnp
        import numpy as np
        key = jax.random.key(seed)
        ks = jax.random.split(key, 5)
        b, n_q, n_kv = (16, 128, 1024)
        query_dim, context_dim, heads, dim_head = (256, 256, 16, 64)
        inner = heads * dim_head
        x = jax.random.normal(ks[0], (b, n_q, query_dim), dtype=jnp.float32)
        context = jax.random.normal(ks[1], (b, n_kv, context_dim), dtype=jnp.float32)
        Wq = jax.random.normal(ks[2], (query_dim, inner), dtype=jnp.float32) * query_dim ** (-0.5)
        Wkv = jax.random.normal(ks[3], (context_dim, 2 * inner), dtype=jnp.float32) * context_dim ** (-0.5)
        Wout = jax.random.normal(ks[4], (inner, query_dim), dtype=jnp.float32) * inner ** (-0.5)
        bout = jnp.zeros((query_dim,), dtype=jnp.float32)
        return {'x': x, 'context': context, 'Wq': Wq, 'Wkv': Wkv, 'Wout': Wout, 'bout': bout}
    _L0_xattn_all = _L0_xattn_setup()
    _L0_xattn_in = {k: v for k, v in _L0_xattn_all.items() if k in ('Wq', 'Wkv', 'Wout', 'bout')}
    del _L0_xattn_all

    def _L0_attn_setup():
        import jax, jax.numpy as jnp
        import numpy as np
        DIM = 256
        NUM_HEAD = 16
        DIM_HEAD = DIM // NUM_HEAD
        RMS_EPS = 1.1920929e-07
        EPS_LIN = 1e-06
        THETA = 10000.0

        def rmsnorm(x, g, eps=RMS_EPS):
            return x * jax.lax.rsqrt(jnp.mean(x * x, axis=-1, keepdims=True) + eps) * g

        def rope_cos_sin(seq_len, dim_head, dtype=jnp.float32):
            inv_freq = 1.0 / THETA ** (jnp.arange(0, dim_head, 2, dtype=dtype) / dim_head)
            t = jnp.arange(seq_len, dtype=dtype)
            freqs = jnp.outer(t, inv_freq)
            return (jnp.cos(freqs), jnp.sin(freqs))

        def apply_rope(t, cos, sin):
            tr = t[..., 0::2]
            ti = t[..., 1::2]
            out_r = tr * cos - ti * sin
            out_i = tr * sin + ti * cos
            return jnp.stack([out_r, out_i], axis=-1).reshape(t.shape)
        key = jax.random.key(seed)
        ks = jax.random.split(key, 5)
        B, L = (4, 1024)
        x = jax.random.normal(ks[0], (B, L, DIM), dtype=jnp.float32)
        Wqkv = jax.random.normal(ks[1], (3 * DIM, DIM), dtype=jnp.float32) * 0.02
        bqkv = jax.random.normal(ks[2], (3 * DIM,), dtype=jnp.float32) * 0.02
        gq = jnp.ones((DIM,), dtype=jnp.float32)
        gk = jnp.ones((DIM,), dtype=jnp.float32)
        Wout = jax.random.normal(ks[3], (DIM, DIM), dtype=jnp.float32) * 0.02
        bout = jax.random.normal(ks[4], (DIM,), dtype=jnp.float32) * 0.02
        gout = jnp.ones((DIM,), dtype=jnp.float32)
        return {'x': x, 'Wqkv': Wqkv, 'bqkv': bqkv, 'gq': gq, 'gk': gk, 'Wout': Wout, 'bout': bout, 'gout': gout}
    _L0_attn_all = _L0_attn_setup()
    _L0_attn_in = {k: v for k, v in _L0_attn_all.items() if k in ('Wqkv', 'bqkv', 'gq', 'gk', 'Wout', 'bout', 'gout')}
    del _L0_attn_all

    def _L0_ffn_setup():
        import jax, jax.numpy as jnp
        import numpy as np
        IN_F = 256
        OUT_F = 256
        B, S = (8, 1024)

        def _pack_ternary(tern):
            enc = (tern + 1.0).astype(jnp.int32).reshape(-1)
            return (enc[0::4] | enc[1::4] << 2 | enc[2::4] << 4 | enc[3::4] << 6).astype(jnp.int32)
        key = jax.random.key(seed)
        kx, kw = jax.random.split(key)
        x = jax.random.normal(kx, (B, S, IN_F), dtype=jnp.float32)
        w = jax.random.normal(kw, (OUT_F, IN_F), dtype=jnp.float32) * 0.02
        scale = jnp.maximum(jnp.mean(jnp.abs(w)), 1e-05)
        wn = w / scale
        tern = jnp.sign(wn) * (jnp.abs(wn) > 0.5).astype(jnp.float32)
        packed = _pack_ternary(tern)
        bias = jnp.zeros((OUT_F,), dtype=jnp.float32)
        return {'x': x, 'packed_weight': packed, 'weight_scale': scale.reshape(1), 'bias': bias}
    _L0_ffn_all = _L0_ffn_setup()
    _L0_ffn_in = {k: v for k, v in _L0_ffn_all.items() if k in ('packed_weight', 'weight_scale', 'bias')}
    del _L0_ffn_all
    return {'x': x, 'ctx_1024': ctx_1024, 'L0_xattn_Wq': _L0_xattn_in['Wq'], 'L0_xattn_Wkv': _L0_xattn_in['Wkv'], 'L0_xattn_Wout': _L0_xattn_in['Wout'], 'L0_xattn_bout': _L0_xattn_in['bout'], 'L0_attn_Wqkv': _L0_attn_in['Wqkv'], 'L0_attn_bqkv': _L0_attn_in['bqkv'], 'L0_attn_gq': _L0_attn_in['gq'], 'L0_attn_gk': _L0_attn_in['gk'], 'L0_attn_Wout': _L0_attn_in['Wout'], 'L0_attn_bout': _L0_attn_in['bout'], 'L0_attn_gout': _L0_attn_in['gout'], 'L0_ffn_packed_weight': _L0_ffn_in['packed_weight'], 'L0_ffn_weight_scale': _L0_ffn_in['weight_scale'], 'L0_ffn_bias': _L0_ffn_in['bias']}

def reference(x, ctx_1024, L0_xattn_Wq, L0_xattn_Wkv, L0_xattn_Wout, L0_xattn_bout, L0_attn_Wqkv, L0_attn_bqkv, L0_attn_gq, L0_attn_gk, L0_attn_Wout, L0_attn_bout, L0_attn_gout, L0_ffn_packed_weight, L0_ffn_weight_scale, L0_ffn_bias):
    import jax
    import jax.numpy as jnp

    def _L0_xattn_ref(x, context, Wq, Wkv, Wout, bout):
        import jax, jax.numpy as jnp
        import numpy as np
        heads, dim_head = (16, 64)
        b, n_q, _ = x.shape
        n_kv = context.shape[1]
        scale = dim_head ** (-0.5)
        q = x @ Wq
        kv = context @ Wkv
        k, v = jnp.split(kv, 2, axis=-1)

        def split_heads(t):
            bb, n, _ = t.shape
            return t.reshape(bb, n, heads, dim_head).transpose(0, 2, 1, 3)
        q, k, v = map(split_heads, (q, k, v))
        i_idx = jnp.arange(n_q)[:, None]
        j_idx = jnp.arange(n_kv)[None, :]
        mask = j_idx % n_q == i_idx
        sim = jnp.einsum('bhid,bhjd->bhij', q, k) * scale
        max_neg = -jnp.finfo(sim.dtype).max
        sim = jnp.where(mask[None, None, :, :], sim, max_neg)
        attn = jax.nn.softmax(sim, axis=-1)
        out = jnp.einsum('bhij,bhjd->bhid', attn, v)
        out = out.transpose(0, 2, 1, 3).reshape(b, n_q, heads * dim_head)
        return out @ Wout + bout

    def _L0_attn_ref(x, Wqkv, bqkv, gq, gk, Wout, bout, gout):
        import jax, jax.numpy as jnp
        import numpy as np
        DIM = 256
        NUM_HEAD = 16
        DIM_HEAD = DIM // NUM_HEAD
        RMS_EPS = 1.1920929e-07
        EPS_LIN = 1e-06
        THETA = 10000.0

        def rmsnorm(x, g, eps=RMS_EPS):
            return x * jax.lax.rsqrt(jnp.mean(x * x, axis=-1, keepdims=True) + eps) * g

        def rope_cos_sin(seq_len, dim_head, dtype=jnp.float32):
            inv_freq = 1.0 / THETA ** (jnp.arange(0, dim_head, 2, dtype=dtype) / dim_head)
            t = jnp.arange(seq_len, dtype=dtype)
            freqs = jnp.outer(t, inv_freq)
            return (jnp.cos(freqs), jnp.sin(freqs))

        def apply_rope(t, cos, sin):
            tr = t[..., 0::2]
            ti = t[..., 1::2]
            out_r = tr * cos - ti * sin
            out_i = tr * sin + ti * cos
            return jnp.stack([out_r, out_i], axis=-1).reshape(t.shape)
        B, L, D = x.shape
        qkv = x @ Wqkv.T + bqkv
        q, k, v = jnp.split(qkv, 3, axis=-1)
        q = rmsnorm(q, gq)
        k = rmsnorm(k, gk)
        split = lambda t: t.reshape(B, L, NUM_HEAD, DIM_HEAD).transpose(0, 2, 1, 3)
        q, k, v = (split(q), split(k), split(v))
        cos, sin = rope_cos_sin(L, DIM_HEAD)
        cos = cos[None, None]
        sin = sin[None, None]
        q = apply_rope(q, cos, sin)
        k = apply_rope(k, cos, sin)
        qf = jax.nn.relu(q)
        kf = jax.nn.relu(k)
        vpad = jnp.concatenate([v, jnp.ones_like(v[..., :1])], axis=-1)
        vk = jnp.einsum('bhlp,bhld->bhpd', vpad, kf)
        res = jnp.einsum('bhpd,bhld->bhlp', vk, qf)
        attn = res[..., :-1] / (res[..., -1:] + EPS_LIN)
        attn = attn.transpose(0, 2, 1, 3).reshape(B, L, D)
        out = rmsnorm(attn @ Wout.T + bout, gout)
        return out

    def _L0_ffn_ref(x, packed_weight, weight_scale, bias):
        import jax, jax.numpy as jnp
        import numpy as np
        IN_F = 256
        OUT_F = 256
        B, S = (8, 1024)

        def _pack_ternary(tern):
            enc = (tern + 1.0).astype(jnp.int32).reshape(-1)
            return (enc[0::4] | enc[1::4] << 2 | enc[2::4] << 4 | enc[3::4] << 6).astype(jnp.int32)
        n = OUT_F * IN_F
        shifts = jnp.array([0, 2, 4, 6], dtype=jnp.int32)
        enc = (packed_weight[None, :] >> shifts[:, None] & 3).reshape(-1)[:n]
        w = (enc.astype(jnp.float32) - 1.0).reshape(OUT_F, IN_F) * weight_scale
        act_scale = 127.0 / jnp.maximum(jnp.max(jnp.abs(x), axis=-1, keepdims=True), 1e-05)
        x_dq = jnp.clip(jnp.round(x * act_scale), -128.0, 127.0) / act_scale
        return jnp.einsum('bsi,oi->bso', x_dq, w) + bias
    x = x + _L0_xattn_ref(_layernorm(x, axis=-1), ctx_1024, L0_xattn_Wq, L0_xattn_Wkv, L0_xattn_Wout, L0_xattn_bout)
    x = x + _L0_attn_ref(_layernorm(x, axis=-1), L0_attn_Wqkv, L0_attn_bqkv, L0_attn_gq, L0_attn_gk, L0_attn_Wout, L0_attn_bout, L0_attn_gout)
    x = x + _L0_ffn_ref(_layernorm(x, axis=-1), L0_ffn_packed_weight, L0_ffn_weight_scale, L0_ffn_bias)
    return x

_drawn_inputs = setup_inputs


def setup_inputs(seed=0):
    import zlib

    import numpy as np

    out = dict(_drawn_inputs(seed))
    spreads = {'L0_xattn_bout': (0.0, 0.1),
     'L0_attn_gq': (1.0, 0.6),
     'L0_attn_gk': (1.0, 0.6),
     'L0_attn_gout': (1.0, 0.2),
     'L0_ffn_bias': (0.0, 0.1)}
    factors = {}
    for name, (base, spread) in spreads.items():
        noise = np.random.default_rng([zlib.crc32(name.encode()), seed]).standard_normal(out[name].shape)
        drawn = base * np.exp(spread * noise) if base else spread * noise
        out[name] = jnp.asarray(drawn.astype(out[name].dtype))
    for name, factor in factors.items():
        out[name] = (out[name] * factor).astype(out[name].dtype)
    return out
```

```python
from contextlib import ExitStack

import numpy as np

import concourse.bass as bass
from concourse import mybir

P = 128
D = 256
KD = D // P
BATCH, NQ, NKV = 32, 32, 257
TILES = BATCH * NQ // P
TB = P // NQ
H, DH = 16, 64
INNER = H * DH
HP = H // 2
GQ = 8
G = NQ // GQ
M = NKV // NQ + 1
MR = M * GQ
KEYS = M * NQ
SH, SD = 16, 16
HH = SH // KD
KVW = P + HH
SCALE = float(DH) ** -0.5
LN_EPS, RMS_EPS, LIN_EPS = 1e-5, 1.1920929e-07, 1e-6
NEG = -1e30
ROUND = float(3 << 22)

F32 = mybir.dt.float32
BF16 = mybir.dt.bfloat16
I32 = mybir.dt.int32
ALU = mybir.AluOpType
ACT = mybir.ActivationFunctionType
X = mybir.AxisListType.X

RING = 3
J_Q, J_QT, J_MIX, J_V, J_O = 2, 8, 8, 2, 1
FRONT = J_Q + J_QT
STEP = FRONT + J_MIX + J_V + J_O
assert STEP % RING == 0

C_ID = 0
C_BD = C_ID + P
C_COS = C_BD + P
C_SIN = C_COS + D
C_EYE = C_SIN + D
C_ABSENT = C_EYE + GQ
C_B = C_ABSENT + G * M
C_H = C_B + TB
C_ROOT = C_H + HH
C_W = C_ROOT + 1


def mix_part(j):
    return j // 4, j // 2 % 2, j % 2


def constants():
    c = np.zeros((P, C_W), np.float32)
    p = np.arange(P)
    c[:, C_ID:C_ID + P] = np.eye(P)
    c[:, C_BD:C_BD + P] = p[:, None] // SD == p[None, :] // SD
    freq = 1.0 / 10000.0 ** (np.arange(0, SD, 2) / SD)
    angle = np.repeat((p % NQ)[:, None] * freq[None, :], 2, axis=1)
    sign = np.where(np.arange(SD) % 2 == 0, 1.0, -1.0)
    root = float(D) ** 0.5
    c[:, C_COS:C_COS + D] = np.tile(np.cos(angle) * root, (1, SH))
    c[:, C_SIN:C_SIN + D] = np.tile(np.sin(angle) * sign * root, (1, SH))
    c[:, C_ROOT] = root
    c[:, C_EYE:C_EYE + GQ] = p[:, None] % GQ == np.arange(GQ)[None, :]
    absent = np.zeros((P, G, M), np.float32)
    absent[:, :, M - 1] = NEG
    absent[p % GQ == 0, 0, M - 1] = 0.0
    c[:, C_ABSENT:C_ABSENT + G * M] = absent.reshape(P, G * M)
    c[:, C_B:C_B + TB] = p[:, None] // NQ == np.arange(TB)[None, :]
    c[:, C_H:C_H + HH] = p[:, None] // SD == np.arange(HH)[None, :]
    return c


def build(nc, a, out):
    with ExitStack() as ctx:
        def sb(name, shape, dt=F32):
            return ctx.enter_context(nc.sbuf_tensor(name, shape, dt))

        def ps(name):
            return ctx.enter_context(nc.psum_tensor(name, [P, 512], F32))

        def sem(name):
            return ctx.enter_context(nc.semaphore(name))

        const = sb("const", [P, C_W])
        ident = const[:, C_ID:C_ID + P]
        same_head = const[:, C_BD:C_BD + P]
        eye8 = const[:, C_EYE:C_EYE + GQ]
        absent = const[:, C_ABSENT:C_ABSENT + G * M]
        of_batch = const[:, C_B:C_B + TB]
        of_head = const[:, C_H:C_H + HH]
        ident16 = sb("ident16", [P, P], BF16)
        wq = sb("wq", [P, KD, INNER])
        wk = sb("wk", [P, H, D])
        wv = sb("wv", [P, KD, INNER])
        wo = sb("wo", [P, HP, D])
        bo = sb("bo", [P, D])
        sw = sb("sw", [P, KD, 3 * D])
        sbias = sb("sbias", [P, 3 * D])
        gains = sb("gains", [P, 2 * D])
        rope_a = sb("rope_a", [P, 2 * D])
        rope_b = sb("rope_b", [P, 2 * D])
        swo = sb("swo", [P, KD, D])
        sbo = sb("sbo", [P, D])
        gout = sb("gout", [P, D])
        packed = sb("packed", [P, KD, 64], I32)
        codes = sb("codes", [P, KD, 4, 64], I32)
        fw = sb("fw", [P, KD, D], BF16)
        wscale = sb("wscale", [P, 1])
        fbias = sb("fbias", [P, D])
        minus_half = sb("minus_half", [P, 2])
        ln_eps = sb("ln_eps", [P, 2])
        rms_eps = sb("rms_eps", [P, 2])

        x_all = sb("x_all", [P, TILES, D])
        keys_t = sb("keys_t", [P, KD, TB, KEYS])
        keys = sb("keys", [P, TB, 2, D])
        key9 = sb("key9", [TB, D])
        ln_stats = sb("ln_stats", [P, 6])
        ln_mv = sb("ln_mv", [P, 2])
        ln_var = sb("ln_var", [P, 1])
        ln_rstd = sb("ln_rstd", [P, 1])
        xn = sb("xn", [P, D])
        xn_t = sb("xn_t", [P, KD, P])
        q_t = sb("q_t", [P, HP, P])
        qt = sb("qt", [P, KD, TB * G, H, GQ])
        masked = sb("masked", [P, 2, G * M, GQ])
        sc = sb("sc", [P, TB * G, M])
        sc_max = sb("sc_max", [P, TB * G])
        sc_off = sb("sc_off", [P, TB * G, M])
        expd = sb("expd", [P, TB * G, M])
        sc_sum = sb("sc_sum", [P, TB * G])
        sc_inv = sb("sc_inv", [P, TB * G])
        prob = sb("prob", [P, TB * G, M])
        spread = sb("spread", [P, TB * G, M - 1, GQ])
        prob9 = sb("prob9", [TB, TB, H])
        prob_t = sb("prob_t", [P, 2 * TB, P])
        mix9 = sb("mix9", [P, KD, TB, H])
        mix = sb("mix", [P, KD, TB, G, H, GQ])
        att_t = sb("att_t", [P, HP, P])
        o_raw = sb("o_raw", [P, D])
        x_bo = sb("x_bo", [P, D])

        x1 = sb("x1", [P, D])
        b_stats = sb("b_stats", [P, 6])
        b_mv = sb("b_mv", [P, 2])
        b_var = sb("b_var", [P, 1])
        b_rstd = sb("b_rstd", [P, 1])
        b_xn = sb("b_xn", [P, D])
        b_xn_t = sb("b_xn_t", [P, KD, P])
        qk = sb("qk", [P, 2 * D])
        v = sb("v", [P, D])
        junk = sb("junk", [P, D])
        sq = sb("sq", [P, 2])
        sq_mean = sb("sq_mean", [P, 2])
        sq_rinv = sb("sq_rinv", [P, 2])
        r_a = sb("r_a", [P, 2 * D])
        r_b = sb("r_b", [P, 2 * D])
        roped = sb("roped", [P, 2 * D])
        feat = sb("feat", [P, 2 * D])
        v_of = sb("v_of", [P, TB, D])
        qf_t = sb("qf_t", [P, KD, P])
        state = sb("state", [P, KD, TB, KVW])
        den = sb("den", [P, KD, HH])
        den_inv = sb("den_inv", [P, KD, HH])
        lin = sb("lin", [P, D])
        lin_t = sb("lin_t", [P, KD, P])
        y = sb("y", [P, D])
        junk_y = sb("junk_y", [P, D])
        y_sq = sb("y_sq", [P, 1])
        y_mean = sb("y_mean", [P, 1])
        y_rinv = sb("y_rinv", [P, 1])
        y_n = sb("y_n", [P, D])
        x2 = sb("x2", [P, D])
        x2_b = sb("x2_b", [P, D])
        f_stats = sb("f_stats", [P, 6])
        f_mv = sb("f_mv", [P, 2])
        f_var = sb("f_var", [P, 1])
        f_rstd = sb("f_rstd", [P, 1])
        f_xn = sb("f_xn", [P, D])
        amax = sb("amax", [P, 1])
        amax_g = sb("amax_g", [P, 1])
        act_inv = sb("act_inv", [P, 1])
        act_scale = sb("act_scale", [P, 1])
        dq = sb("dq", [P, 1])
        dq_w = sb("dq_w", [P, 1])
        f_q = sb("f_q", [P, D])
        f_r = sb("f_r", [P, D])
        f_i = sb("f_i", [P, D], BF16)
        f_t = sb("f_t", [P, KD, P], BF16)
        x3 = sb("x3", [P, D])

        ring = [ps(f"ring{i}") for i in range(RING)]
        ps_s = [ps(f"ps_s{i}") for i in range(2)]
        ps_x, ps_y, ps_z = ps("ps_x"), ps("ps_y"), ps("ps_z")

        names = """x0_in x_in const_in wq_in wk_in wv_in wo_in self_in ffn_in keys_t_in keys_in
            zeros_set pads_set half_set ident16_set rope_set codes_set fw_set
            ln_stats_first ln_stats_set ln_mv_set ln_var_set ln_rstd_set xn_set xn_t_filled xn_t_set
            ring_filled ring_drained
            scores_filled masked_set scores_drained sc_set sc_added max_set off_set exp_set sum_set inv_set prob_set spread_set
            prob9_filled prob9_set prob_t_filled prob_t_set mix9_filled mix9_set mix_set x_bo_set x1_set
            b_stats_set b_mv_set b_var_set b_rstd_set b_xn_set b_xn_t_filled b_xn_t_set
            qkv_filled qk_set v_set sq_set sq_mean_set sq_rinv_set r_ab_set roped_set feat_set v_of_set
            kv_filled qf_t_set state_set num_filled den_set den_inv_set lin_set lin_t_filled lin_t_set
            y_filled y_set y_sq_set y_mean_set y_rinv_set y_n_set x2_set x2_b_set
            f_stats_set f_mv_set f_var_set f_rstd_set f_xn_set amax_set amax_g_set act_inv_set act_scale_set
            dq_set dq_w_set f_q_set f_r_set f_i_set f_t_filled f_t_set f_filled x3_set out_stored""".split()
        s = {n: sem(n) for n in names}

        block = ctx.enter_context(nc.Block())

        @block.sync
        def _(sp):
            def load_keys_t(t):
                sp.dma_start(keys_t[:, :, :, 0:NKV].rearrange("p k b j -> p (k b) j"),
                             a["ctx_t"][t]).then_inc(s["keys_t_in"], 16)

            def load_keys(t):
                sp.dma_start(keys[:, :, :, :], a["ctx_k"][t]).then_inc(s["keys_in"], 16)
                sp.dma_start(key9[:, :], a["ctx_9"][t]).then_inc(s["keys_in"], 16)

            x_v = a["x"].rearrange("(t p) d -> p t d", p=P)
            sp.dma_start(x_all[:, 0, :], x_v[:, 0, :]).then_inc(s["x0_in"], 16)
            sp.dma_start(const[:, :], a["const"]).then_inc(s["const_in"], 16)
            sp.dma_start(wq[:, :, :], a["wq"].rearrange("(k p) n -> p k n", p=P)).then_inc(s["wq_in"], 16)
            for half in range(2):
                rows = slice(half * DH, (half + 1) * DH)
                sp.dma_start(wk[rows, half:H:2, :],
                             a["wk_t"].rearrange("(c r) d -> r c d", r=P)[rows, :, :]).then_inc(s["wk_in"], 16)
            load_keys_t(0)
            sp.dma_start(x_all[:, 1:TILES, :], x_v[:, 1:TILES, :]).then_inc(s["x_in"], 16)
            load_keys(0)
            sp.dma_start(wv[:, :, :], a["wv"].rearrange("(k p) n -> p k n", p=P)).then_inc(s["wv_in"], 16)
            sp.dma_start(wo[:, :, :], a["wo"].rearrange("(c p) n -> p c n", p=P)).then_inc(s["wo_in"], 16)

            def stores(t):
                sp.wait_ge(s["x3_set"], t + 1)
                sp.dma_start(out[t], x3[:, :]).then_inc(s["out_stored"], 16)

            def step(t, back):
                sp.wait_ge(s["scores_filled"], TB * t + TB)
                load_keys_t(t + 1)
                sp.wait_ge(s["ring_filled"], STEP * t + FRONT + FRONT + J_MIX)
                load_keys(t + 1)
                if back:
                    stores(t - 1)

            step(0, False)
            with sp.Fori(1, TILES - 1) as t:
                step(t, True)
            stores(TILES - 2)
            stores(TILES - 1)
            sp.wait_ge(s["out_stored"], 16 * TILES)

        @block.tensor
        def _(pe):
            mm = nc.tensor.matmul

            def ring_job(n, phase, c):
                if isinstance(n, int) and n + c < RING:
                    return ring[(phase + c) % RING]
                pe.wait_ge(s["ring_drained"], n + (c - RING + 1))
                return ring[(phase + c) % RING]

            def transpose_xn(t, first=False):
                pe.wait_ge(s["xn_set"], t + 1)
                for k in range(KD):
                    last = nc.tensor.transpose(ps_z[:, k * P:(k + 1) * P], xn[:, k * P:(k + 1) * P], ident)
                last.then_inc(s["xn_t_filled"], 1)

            def q_jobs(t, n, phase):
                pe.wait_ge(s["xn_t_set"], t + 1)
                for j in range(J_Q):
                    bank = ring_job(n, phase, j)
                    for c in range(4):
                        hp = 4 * j + c
                        for k in range(KD):
                            last = mm(bank[:, c * P:(c + 1) * P], wq[:, k, hp * P:(hp + 1) * P], xn_t[:, k, :],
                                      start=(k == 0), stop=(k == KD - 1))
                    last.then_inc(s["ring_filled"], 1)

            def qt_jobs(n, phase, jobs):
                for j in jobs:
                    heads, k = j // KD, j % KD
                    bank = ring_job(n, phase, J_Q + j)
                    pe.wait_ge(s["ring_drained"], n + 1 + (4 * heads + 3) // 8)
                    for c in range(4):
                        h = 4 * heads + c
                        last = mm(bank[:, c * P:(c + 1) * P], wk[:, h, k * P:(k + 1) * P], q_t[:, h // 2, :],
                                  start=True, stop=True)
                    last.then_inc(s["ring_filled"], 1)

            def scores(t, batches):
                for b in batches:
                    if b == 0:
                        pe.wait_ge(s["keys_t_in"], 16 * t + 16)
                    if b >= 2:
                        pe.wait_ge(s["scores_drained"], TB * t + b - 1)
                    elif not (isinstance(t, int) and t == 0):
                        pe.wait_ge(s["prob_t_set"], 2 * t + b - 1)
                    for g in range(G):
                        for k in range(KD):
                            last = mm(ps_s[b % 2][:, g * MR:(g + 1) * MR],
                                      qt[:, k, b * G + g, :, :].rearrange("p h q -> p (h q)"),
                                      keys_t[:, k, b, :].rearrange("p (m q) -> p m q", m=M)[:, :, g * GQ:(g + 1) * GQ],
                                      start=(k == 0), stop=(k == KD - 1))
                    last.then_inc(s["scores_filled"], 1)

            def transpose_prob(t):
                pe.wait_ge(s["prob_set"], t + 1)
                mm(ps_z[0:TB, 0:H], prob[:, 0:TB * G:G, M - 1], ident[:, 0:P:GQ], start=True, stop=True)\
                    .then_inc(s["prob9_filled"], 1)
                for j in range(2):
                    pe.wait_ge(s["spread_set"], 2 * t + j + 1)
                    pe.wait_ge(s["scores_drained"], TB * t + 3 + j)
                    for c in range(4):
                        pair = 4 * j + c
                        last = nc.tensor.transpose(ps_s[j][:, c * P:(c + 1) * P],
                                                   spread[:, 2 * pair:2 * pair + 2, :, :].rearrange("p g m r -> p (g m r)"),
                                                   ident)
                    last.then_inc(s["prob_t_filled"], 1)

            def mix9_job(t):
                pe.wait_ge(s["prob9_set"], t + 1)
                pe.wait_ge(s["keys_in"], 32 * t + 32)
                for k in range(KD):
                    last = mm(ps_z[:, k * TB * H:(k + 1) * TB * H], key9[:, k * P:(k + 1) * P],
                              prob9[:, :, :], start=True, stop=True)
                last.then_inc(s["mix9_filled"], 1)

            def mix_jobs(t, n, phase, jobs):
                for j in jobs:
                    b2, k, half = mix_part(j)
                    rows = slice(half * 64, half * 64 + 64)
                    bank = ring_job(n, phase, j)
                    pe.wait_ge(s["prob_t_set"], 2 * t + 1 + b2)
                    for c in range(4):
                        b, g2 = 2 * b2 + c // 2, c % 2
                        last = mm(bank[:, c * P:(c + 1) * P], keys[rows, b, g2, k * P:(k + 1) * P],
                                  prob_t[rows, 2 * b + g2, :], start=True, stop=True)
                    last.then_inc(s["ring_filled"], 1)

            def value_jobs(t, n, phase):
                pe.wait_ge(s["mix_set"], t + 1)
                for j in range(J_V):
                    bank = ring_job(n, phase, j)
                    for c in range(4):
                        for k in range(KD):
                            for half in range(2):
                                h = 2 * (4 * j + c) + half
                                last = mm(bank[half * DH:(half + 1) * DH, c * P:(c + 1) * P],
                                          wv[:, k, h * DH:(h + 1) * DH],
                                          mix[:, k, :, :, h, :].rearrange("p b g q -> p (b g) q"),
                                          start=(k == 0), stop=(k == KD - 1), skip_group_check=True)
                    last.then_inc(s["ring_filled"], 1)

            def out_job(n, phase, drained):
                bank = ring_job(n, phase, 0)
                pe.wait_ge(s["ring_drained"], drained)
                for c in range(HP):
                    last = mm(bank[:, 0:D], att_t[:, c, :], wo[:, c, :], start=(c == 0), stop=(c == HP - 1))
                last.then_inc(s["ring_filled"], 1)

            def back_xn(u):
                pe.wait_ge(s["b_xn_set"], u + 1)
                for k in range(KD):
                    last = nc.tensor.transpose(ps_z[:, k * P:(k + 1) * P], b_xn[:, k * P:(k + 1) * P], ident)
                last.then_inc(s["b_xn_t_filled"], 1)

            def back_qkv(u):
                pe.wait_ge(s["b_xn_t_set"], u + 1)
                for bank, at, width in ((ps_x, 0, 2 * D), (ps_y, 2 * D, D)):
                    for k in range(KD):
                        last = mm(bank[:, 0:width], b_xn_t[:, k, :], sw[:, k, at:at + width],
                                  start=(k == 0), stop=(k == KD - 1))
                last.then_inc(s["qkv_filled"], 1)

            def back_kv(u):
                pe.wait_ge(s["feat_set"], 2 * u + 2)
                pe.wait_ge(s["v_of_set"], u + 1)
                for k in range(KD):
                    nc.tensor.transpose(ps_z[:, k * P:(k + 1) * P], feat[:, k * P:(k + 1) * P], ident)
                    kf = feat[:, D + k * P:D + (k + 1) * P]
                    mm((ps_x, ps_y)[k][:, :], kf, v_of[:, :, k * P:(k + 1) * P], start=True, stop=True)
                    last = mm(ps_z[:, D + k * TB:D + (k + 1) * TB], kf, of_batch, start=True, stop=True)
                last.then_inc(s["kv_filled"], 1)

            def back_num(u):
                pe.wait_ge(s["qf_t_set"], u + 1)
                pe.wait_ge(s["state_set"], 4 * u + 4)
                for k in range(KD):
                    for b in range(TB):
                        last = mm(ps_x[b * NQ:(b + 1) * NQ, k * KVW:(k + 1) * KVW], qf_t[:, k, b * NQ:(b + 1) * NQ],
                                  state[:, k, b, :], start=True, stop=True)
                last.then_inc(s["num_filled"], 1)

            def back_lin(u):
                pe.wait_ge(s["lin_set"], u + 1)
                for k in range(KD):
                    last = nc.tensor.transpose(ps_z[:, k * P:(k + 1) * P], lin[:, k * P:(k + 1) * P], ident)
                last.then_inc(s["lin_t_filled"], 1)

            def back_out(u):
                pe.wait_ge(s["lin_t_set"], u + 1)
                for k in range(KD):
                    last = mm(ps_y[:, 0:D], lin_t[:, k, :], swo[:, k, :], start=(k == 0), stop=(k == KD - 1))
                last.then_inc(s["y_filled"], 1)

            def back_quant(u):
                pe.wait_ge(s["f_i_set"], u + 1)
                for k in range(KD):
                    last = nc.tensor.transpose(ps_z[:, k * 64:(k + 1) * 64].bitcast(BF16),
                                               f_i[:, k * P:(k + 1) * P], ident16[:, :])
                last.then_inc(s["f_t_filled"], 1)

            def back_ffn(u):
                pe.wait_ge(s["f_t_set"], u + 1)
                for k in range(KD):
                    last = mm(ps_x[:, 0:D], f_t[:, k, :], fw[:, k, :], start=(k == 0), stop=(k == KD - 1))
                last.then_inc(s["f_filled"], 1)

            def step(t, front, back):
                u = t - 1
                n, phase = STEP * t + FRONT, FRONT
                scores(t, (0, 1))
                if front:
                    transpose_xn(t + 1)
                scores(t, (2,))
                if back:
                    if front:
                        pe.wait_ge(s["xn_t_set"], t + 2)
                    back_xn(u)
                scores(t, (3,))
                if front:
                    q_jobs(t + 1, n, phase)
                if back:
                    back_qkv(u)
                if front:
                    qt_jobs(n, phase, range(0, 6))
                if back:
                    back_kv(u)
                if front:
                    qt_jobs(n, phase, range(6, J_QT))
                    n, phase = n + FRONT, phase + FRONT
                if back:
                    back_num(u)
                elif front:
                    pe.wait_ge(s["xn_t_set"], t + 2)
                transpose_prob(t)
                mix9_job(t)
                mix_jobs(t, n, phase, range(0, 3))
                if back:
                    pe.wait_ge(s["mix9_set"], t + 1)
                    back_lin(u)
                mix_jobs(t, n, phase, range(3, 5))
                if back:
                    back_out(u)
                mix_jobs(t, n, phase, range(5, J_MIX))
                value_jobs(t, n + J_MIX, phase + J_MIX)
                if back:
                    back_quant(u)
                out_job(n + J_MIX + J_V, phase + J_MIX + J_V, n + J_MIX + J_V)
                if back:
                    back_ffn(u)

            pe.wait_ge(s["const_in"], 16)
            transpose_xn(0)
            pe.wait_ge(s["wq_in"], 16)
            q_jobs(0, 0, 0)
            pe.wait_ge(s["wk_in"], 32)
            pe.wait_ge(s["zeros_set"], 2)
            qt_jobs(0, 0, range(J_QT))
            pe.wait_ge(s["ring_drained"], FRONT)
            pe.wait_ge(s["pads_set"], 1)
            pe.wait_ge(s["wv_in"], 16)
            pe.wait_ge(s["wo_in"], 16)
            step(0, True, False)
            pe.wait_ge(s["self_in"], 16 * 7)
            pe.wait_ge(s["ident16_set"], 1)
            pe.wait_ge(s["fw_set"], 1)
            with pe.Fori(1, TILES - 1) as t:
                step(t, True, True)
            step(TILES - 1, False, True)
            u = TILES - 1
            for stage in (back_xn, back_qkv, back_kv, back_num, back_lin, back_out, back_quant, back_ffn):
                stage(u)

        @block.scalar
        def _(act):
            def copy(o, i):
                return nc.scalar.activation(o, i, ACT.Copy)

            def drain(n, c, o, i):
                act.wait_ge(s["ring_filled"], n + (c + 1))
                copy(o, i).then_inc(s["ring_drained"], 1)

            def drain_xn(t):
                act.wait_ge(s["xn_t_filled"], t + 1)
                copy(xn_t[:, :, :], ps_z[:, 0:D]).then_inc(s["xn_t_set"], 1)

            def drain_q(n, phase):
                for j in range(J_Q):
                    drain(n, j, q_t[:, 4 * j:4 * j + 4, :], ring[(phase + j) % RING][:, :])

            def drain_qt(n, phase, jobs):
                for j in jobs:
                    heads, k = j // KD, j % KD
                    drain(n, J_Q + j, qt[:, k, :, 4 * heads:4 * heads + 4, :].rearrange("p g h q -> p h g q"),
                          ring[(phase + J_Q + j) % RING][:, :].rearrange("p (h g q) -> p h g q", h=4, q=GQ))

            def exponentials(t):
                act.wait_ge(s["off_set"], t + 1)
                nc.scalar.activation(expd[:, :, :], sc_off[:, :, :], ACT.Exp, scale=SCALE).then_inc(s["exp_set"], 1)

            def drain_mix(n, phase, jobs):
                for j in jobs:
                    b2, k, half = mix_part(j)
                    drain(n, j, mix[:, k, 2 * b2:2 * b2 + 2, half:G:2, :, :].rearrange("p b g h q -> p b g (h q)"),
                          ring[(phase + j) % RING][:, :].rearrange("p (b g n) -> p b g n", b=2, g=2))

            def drain_values(n, phase):
                for j in range(J_V):
                    drain(n, j, att_t[:, 4 * j:4 * j + 4, :], ring[(phase + j) % RING][:, :])

            def drain_mix9(t):
                act.wait_ge(s["mix9_filled"], t + 1)
                copy(mix9[:, :, :, :], ps_z[:, 0:KD * TB * H]).then_inc(s["mix9_set"], 1)

            def back_xn(u):
                act.wait_ge(s["b_xn_t_filled"], u + 1)
                copy(b_xn_t[:, :, :], ps_z[:, 0:D]).then_inc(s["b_xn_t_set"], 1)

            def back_squares(u):
                act.wait_ge(s["qk_set"], u + 1)
                for i in range(2):
                    if i:
                        act.wait_ge(s["sq_set"], 2 * u + 1)
                    elif not (isinstance(u, int) and u == 0):
                        act.wait_ge(s["sq_set"], 2 * u)
                    nc.scalar.activation(junk[:, :], qk[:, i * D:(i + 1) * D], ACT.Square,
                                         accum_out=sq[:, i:i + 1]).then_inc(s["sq_set"], 1)

            def back_relu(u):
                act.wait_ge(s["roped_set"], u + 1)
                act.wait_ge(s["sq_rinv_set"], u + 1)
                for i in range(2):
                    nc.scalar.activation(feat[:, i * D:(i + 1) * D], roped[:, i * D:(i + 1) * D], ACT.Relu,
                                         scale=sq_rinv[:, i:i + 1]).then_inc(s["feat_set"], 1)

            def back_qf(u):
                act.wait_ge(s["kv_filled"], u + 1)
                copy(qf_t[:, :, :], ps_z[:, 0:D]).then_inc(s["qf_t_set"], 1)

            def back_lin(u):
                act.wait_ge(s["lin_t_filled"], u + 1)
                copy(lin_t[:, :, :], ps_z[:, 0:D]).then_inc(s["lin_t_set"], 1)

            def back_y(u):
                act.wait_ge(s["y_set"], u + 1)
                nc.scalar.activation(junk_y[:, :], y[:, :], ACT.Square, accum_out=y_sq[:, :]).then_inc(s["y_sq_set"], 1)

            def back_quant(u):
                act.wait_ge(s["f_t_filled"], u + 1)
                copy(f_t[:, :, :], ps_z[:, 0:P].bitcast(BF16)).then_inc(s["f_t_set"], 1)

            def step(t, front, back):
                u = t - 1
                n, phase = STEP * t + FRONT, FRONT
                if front:
                    drain_xn(t + 1)
                if back:
                    back_xn(u)
                if front:
                    drain_q(n, phase)
                if back:
                    back_squares(u)
                exponentials(t)
                if front:
                    drain_qt(n, phase, range(0, 4))
                if back:
                    back_relu(u)
                if front:
                    drain_qt(n, phase, range(4, 6))
                if back:
                    back_qf(u)
                if front:
                    drain_qt(n, phase, range(6, J_QT))
                    n, phase = n + FRONT, phase + FRONT
                drain_mix9(t)
                drain_mix(n, phase, range(0, 3))
                if back:
                    back_lin(u)
                drain_mix(n, phase, range(3, 5))
                if back:
                    back_y(u)
                drain_mix(n, phase, range(5, J_MIX))
                drain_values(n + J_MIX, phase + J_MIX)
                if back:
                    back_quant(u)
                drain(n + J_MIX + J_V, 0, o_raw[:, :], ring[(phase + J_MIX + J_V) % RING][:, 0:D])

            def broadcast(o, name, w):
                act.dma_start(o, a[name].rearrange("(o n) -> o n", o=1).to_broadcast([P, w])).then_inc(s["self_in"], 16)

            act.dma_start(sw[:, :, :], a["swqkv_t"].rearrange("(k p) n -> p k n", p=P)).then_inc(s["self_in"], 16)
            act.dma_start(swo[:, :, :], a["swo_t"].rearrange("(k p) n -> p k n", p=P)).then_inc(s["self_in"], 16)
            broadcast(sbias[:, :], "sbqkv", 3 * D)
            broadcast(gains[:, 0:D], "sgq", D)
            broadcast(gains[:, D:2 * D], "sgk", D)
            broadcast(sbo[:, :], "sbo", D)
            broadcast(gout[:, :], "sgout", D)
            for o, name, w in ((bo, "bo", D), (fbias, "fbias", D), (wscale, "wscale", 1)):
                act.dma_start(o[:, :], a[name].rearrange("(o n) -> o n", o=1).to_broadcast([P, w]))\
                    .then_inc(s["ffn_in"], 16)
            act.dma_start(packed[:, :, :], a["packed_t"].rearrange("(k p) n -> p k n", p=P)).then_inc(s["ffn_in"], 16)

            drain_xn(0)
            drain_q(0, 0)
            drain_qt(0, 0, range(J_QT))
            step(0, True, False)
            with act.Fori(1, TILES - 1) as t:
                step(t, True, True)
            step(TILES - 1, False, True)
            u = TILES - 1
            for stage in (back_xn, back_squares, back_relu, back_qf, back_lin, back_y, back_quant):
                stage(u)

        @block.vector
        def _(dve):
            V = nc.vector

            def normalise(t1, src, stats, stats_s, count, mv, mv_s, rstd, rstd_s, o, o_s):
                V.bn_stats(stats[:, :], src).then_inc(s[stats_s], 1)
                dve.wait_ge(s[stats_s], 1)
                dve.wait_ge(s[stats_s], count)
                V.bn_aggr(mv[:, :], stats[:, :]).then_inc(s[mv_s], 1)
                dve.wait_ge(s[rstd_s], t1)
                V.tensor_scalar(o, src, mv[:, 0:1], rstd[:, 0:1], ALU.subtract, ALU.mult).then_inc(s[o_s], 1)

            def norm_front(t):
                if not (isinstance(t, int) and t == 0):
                    dve.wait_ge(s["xn_t_filled"], t)
                stats_s, count = ("ln_stats_first", t + 1) if isinstance(t, int) else ("ln_stats_set", t - 1)
                normalise(t + 1, x_all[:, t, :], ln_stats, stats_s, count, ln_mv, "ln_mv_set",
                          ln_rstd, "ln_rstd_set", xn[:, :], "xn_set")

            def take_scores(t, batches):
                for b in batches:
                    dve.wait_ge(s["scores_filled"], TB * t + b + 1)
                    V.tensor_tensor(masked[:, b % 2, :, :],
                                    ps_s[b % 2][:, 0:G * MR].rearrange("p (m r) -> p m r", r=GQ),
                                    eye8.unsqueeze(1).to_broadcast([P, G * M, GQ]), ALU.mult)\
                        .then_inc(s["scores_drained"], 1)
                    dve.wait_ge(s["scores_drained"], TB * t + b + 1)
                    V.tensor_reduce(sc[:, b * G:(b + 1) * G, :].rearrange("p g m -> p (g m)"),
                                    masked[:, b % 2, :, :], X, ALU.add).then_inc(s["sc_set"], 1)

            def softmax_off(t):
                dve.wait_ge(s["sc_set"], TB * t + TB)
                V.tensor_tensor(sc[:, :, :].rearrange("p (b g) m -> p b (g m)", b=TB),
                                sc[:, :, :].rearrange("p (b g) m -> p b (g m)", b=TB),
                                absent.unsqueeze(1).to_broadcast([P, TB, G * M]), ALU.add).then_inc(s["sc_added"], 1)
                dve.wait_ge(s["sc_added"], t + 1)
                V.tensor_reduce(sc_max[:, :], sc[:, :, :], X, ALU.max).then_inc(s["max_set"], 1)
                dve.wait_ge(s["max_set"], t + 1)
                V.tensor_tensor(sc_off[:, :, :], sc[:, :, :],
                                sc_max[:, :].unsqueeze(2).to_broadcast([P, TB * G, M]), ALU.subtract)\
                    .then_inc(s["off_set"], 1)

            def softmax_prob(t):
                dve.wait_ge(s["exp_set"], t + 1)
                V.tensor_reduce(sc_sum[:, :], expd[:, :, :], X, ALU.add).then_inc(s["sum_set"], 1)
                dve.wait_ge(s["sum_set"], t + 1)
                V.reciprocal(sc_inv[:, :], sc_sum[:, :]).then_inc(s["inv_set"], 1)
                dve.wait_ge(s["inv_set"], t + 1)
                V.tensor_tensor(prob[:, :, :], expd[:, :, :],
                                sc_inv[:, :].unsqueeze(2).to_broadcast([P, TB * G, M]), ALU.mult)\
                    .then_inc(s["prob_set"], 1)
                dve.wait_ge(s["prob_set"], t + 1)
                for j in range(2):
                    at = slice(8 * j, 8 * j + 8)
                    V.tensor_tensor(spread[:, at, :, :],
                                    prob[:, at, 0:M - 1].unsqueeze(3).to_broadcast([P, 8, M - 1, GQ]),
                                    eye8.unsqueeze(1).unsqueeze(1).to_broadcast([P, 8, M - 1, GQ]), ALU.mult)\
                        .then_inc(s["spread_set"], 1)

            def take_prob_t(t):
                dve.wait_ge(s["prob9_filled"], t + 1)
                V.tensor_tensor(prob9[:, :, :], ps_z[0:TB, 0:H].unsqueeze(1).to_broadcast([TB, TB, H]),
                                ident[0:TB, 0:TB].unsqueeze(2).to_broadcast([TB, TB, H]), ALU.mult)\
                    .then_inc(s["prob9_set"], 1)
                for j in range(2):
                    dve.wait_ge(s["prob_t_filled"], 2 * t + j + 1)
                    V.tensor_copy(prob_t[:, 4 * j:4 * j + 4, :], ps_s[j][:, :]).then_inc(s["prob_t_set"], 1)

            def back_norm(u):
                dve.wait_ge(s["x1_set"], u + 1)
                normalise(u + 1, x1[:, :], b_stats, "b_stats_set", u + 1, b_mv, "b_mv_set",
                          b_rstd, "b_rstd_set", b_xn[:, :], "b_xn_set")

            def back_bias(u):
                dve.wait_ge(s["qkv_filled"], u + 1)
                V.tensor_tensor(qk[:, :], ps_x[:, :], sbias[:, 0:2 * D], ALU.add).then_inc(s["qk_set"], 1)
                V.tensor_tensor(v[:, :], ps_y[:, 0:D], sbias[:, 2 * D:3 * D], ALU.add).then_inc(s["v_set"], 1)

            def back_rope(u):
                dve.wait_ge(s["r_ab_set"], 2 * u + 2)
                rb = r_b[:, :].rearrange("p (n two) -> p n two", two=2)
                V.tensor_tensor(roped[:, :].rearrange("p (n two) -> p n two", two=2),
                                r_a[:, :].rearrange("p (n two) -> p n two", two=2),
                                rb[:, :, ::-1], ALU.add).then_inc(s["roped_set"], 1)

            def back_state(u):
                dve.wait_ge(s["kv_filled"], u + 1)
                for k in range(KD):
                    V.tensor_tensor(state[:, k, :, 0:P], (ps_x, ps_y)[k][:, :].rearrange("p (b e) -> p b e", b=TB),
                                    same_head.unsqueeze(1).to_broadcast([P, TB, P]), ALU.mult)\
                        .then_inc(s["state_set"], 1)
                dve.wait_ge(s["qf_t_set"], u + 1)
                for k in range(KD):
                    V.tensor_tensor(state[:, k, :, P:KVW],
                                    ps_z[:, D + k * TB:D + (k + 1) * TB].unsqueeze(2).to_broadcast([P, TB, HH]),
                                    of_head.unsqueeze(1).to_broadcast([P, TB, HH]), ALU.mult)\
                        .then_inc(s["state_set"], 1)

            def back_lin(u):
                dve.wait_ge(s["num_filled"], u + 1)
                num = ps_x[:, 0:KD * KVW].rearrange("p (k e) -> p k e", k=KD)
                V.tensor_scalar(den[:, :, :], num[:, :, P:KVW], LIN_EPS, None, ALU.add).then_inc(s["den_set"], 1)
                dve.wait_ge(s["den_set"], u + 1)
                V.reciprocal(den_inv[:, :, :], den[:, :, :]).then_inc(s["den_inv_set"], 1)
                dve.wait_ge(s["den_inv_set"], u + 1)
                for k in range(KD):
                    ins = V.tensor_tensor(lin[:, k * P:(k + 1) * P].rearrange("p (h e) -> p h e", e=SD),
                                          num[:, k, 0:P].rearrange("p (h e) -> p h e", e=SD),
                                          den_inv[:, k, :].unsqueeze(2).to_broadcast([P, HH, SD]), ALU.mult)
                ins.then_inc(s["lin_set"], 1)

            def back_y(u):
                dve.wait_ge(s["y_filled"], u + 1)
                V.tensor_tensor(y[:, :], ps_y[:, 0:D], sbo[:, :], ALU.add).then_inc(s["y_set"], 1)

            def back_x2(u):
                dve.wait_ge(s["y_rinv_set"], u + 1)
                V.scalar_tensor_tensor(y_n[:, :], y[:, :], y_rinv[:, 0:1], gout[:, :], ALU.mult, ALU.mult)\
                    .then_inc(s["y_n_set"], 1)
                dve.wait_ge(s["y_n_set"], u + 1)
                V.tensor_tensor(x2[:, :], x1[:, :], y_n[:, :], ALU.add).then_inc(s["x2_set"], 1)
                dve.wait_ge(s["x2_set"], u + 1)
                normalise(u + 1, x2[:, :], f_stats, "f_stats_set", u + 1, f_mv, "f_mv_set",
                          f_rstd, "f_rstd_set", f_xn[:, :], "f_xn_set")

            def back_quant(u):
                dve.wait_ge(s["f_xn_set"], u + 1)
                V.tensor_reduce(amax[:, :], f_xn[:, :], X, ALU.max, apply_absolute_value=True).then_inc(s["amax_set"], 1)
                dve.wait_ge(s["amax_set"], u + 1)
                V.tensor_scalar(amax_g[:, :], amax[:, :], 1e-5, None, ALU.max).then_inc(s["amax_g_set"], 1)
                dve.wait_ge(s["amax_g_set"], u + 1)
                V.reciprocal(act_inv[:, :], amax_g[:, :]).then_inc(s["act_inv_set"], 1)
                dve.wait_ge(s["act_inv_set"], u + 1)
                V.tensor_scalar(act_scale[:, :], act_inv[:, :], 127.0, None, ALU.mult).then_inc(s["act_scale_set"], 1)
                dve.wait_ge(s["act_scale_set"], u + 1)
                V.tensor_scalar(f_q[:, :], f_xn[:, :], act_scale[:, 0:1], -128.0, ALU.mult, ALU.max)\
                    .then_inc(s["f_q_set"], 1)
                V.reciprocal(dq[:, :], act_scale[:, :]).then_inc(s["dq_set"], 1)
                dve.wait_ge(s["f_q_set"], u + 1)
                V.tensor_scalar(f_r[:, :], f_q[:, :], 127.0, ROUND, ALU.min, ALU.add).then_inc(s["f_r_set"], 1)
                dve.wait_ge(s["dq_set"], u + 1)
                V.tensor_tensor(dq_w[:, :], dq[:, :], wscale[:, :], ALU.mult).then_inc(s["dq_w_set"], 1)
                dve.wait_ge(s["f_r_set"], u + 1)
                V.tensor_scalar(f_i[:, :], f_r[:, :], -ROUND, None, ALU.add).then_inc(s["f_i_set"], 1)

            def back_x3(u):
                dve.wait_ge(s["f_filled"], u + 1)
                dve.wait_ge(s["dq_w_set"], u + 1)
                dve.wait_ge(s["x2_b_set"], u + 1)
                if not (isinstance(u, int) and u == 0):
                    dve.wait_ge(s["out_stored"], 16 * u)
                V.scalar_tensor_tensor(x3[:, :], ps_x[:, 0:D], dq_w[:, 0:1], x2_b[:, :], ALU.mult, ALU.add)\
                    .then_inc(s["x3_set"], 1)

            def step(t, front, back):
                u = t - 1
                if front:
                    norm_front(t + 1)
                if back:
                    back_norm(u)
                take_scores(t, (0, 1, 2, 3))
                softmax_off(t)
                if back:
                    back_bias(u)
                softmax_prob(t)
                if back:
                    back_rope(u)
                    back_state(u)
                    back_lin(u)
                take_prob_t(t)
                if back:
                    back_y(u)
                    back_x2(u)
                    back_quant(u)
                    back_x3(u)

            dve.wait_ge(s["x0_in"], 16)
            norm_front(0)
            dve.wait_ge(s["const_in"], 16)
            V.tensor_copy(ident16[:, :], ident).then_inc(s["ident16_set"], 1)
            dve.wait_ge(s["ffn_in"], 64)
            for c in range(4):
                V.tensor_scalar(codes[:, :, c, :], packed[:, :, :], 2 * c, 3, ALU.logical_shift_right,
                                ALU.bitwise_and).then_inc(s["codes_set"], 1)
            dve.wait_ge(s["codes_set"], 4)
            V.tensor_scalar(fw[:, :, :].rearrange("p k n -> p (k n)"), codes[:, :, :, :].rearrange("p k c n -> p (k c n)"),
                            -1.0, None, ALU.add).then_inc(s["fw_set"], 1)
            dve.wait_ge(s["x_in"], 16)
            step(0, True, False)
            dve.wait_ge(s["self_in"], 16 * 7)
            dve.wait_ge(s["rope_set"], 5)
            with dve.Fori(1, TILES - 1) as t:
                step(t, True, True)
            step(TILES - 1, False, True)
            u = TILES - 1
            for stage in (back_norm, back_bias, back_rope, back_state, back_lin, back_y, back_x2, back_quant, back_x3):
                stage(u)

        @block.gpsimd
        def _(pool):
            g = nc.gpsimd

            def rsqrt(t1, o, o_s, mean, mean_s, src, src_s, count, eps, n=1):
                pool.wait_ge(s[src_s], count * t1)
                g.tensor_tensor(mean, src, eps[:, 0:n], ALU.add).then_inc(s[mean_s], 1)
                pool.wait_ge(s[mean_s], t1)
                g.tensor_tensor(o, mean, minus_half[:, 0:n], ALU.pow).then_inc(s[o_s], 1)

            def norm_front(t):
                rsqrt(t + 1, ln_rstd[:, :], "ln_rstd_set", ln_var[:, :], "ln_var_set", ln_mv[:, 1:2], "ln_mv_set",
                      1, ln_eps)

            def add_mix9(t, drained):
                pool.wait_ge(s["mix9_set"], t + 1)
                pool.wait_ge(s["ring_drained"], drained)
                for k in range(KD):
                    at = mix[:, k, :, 0, :, 0]
                    ins = g.tensor_tensor(at, at, mix9[:, k, :, :], ALU.add)
                ins.then_inc(s["mix_set"], 1)

            def residual(t, drained):
                g.tensor_tensor(x_bo[:, :], x_all[:, t, :], bo[:, :], ALU.add).then_inc(s["x_bo_set"], 1)
                pool.wait_ge(s["x_bo_set"], t + 1)
                pool.wait_ge(s["ring_drained"], drained)
                g.tensor_tensor(x1[:, :], x_bo[:, :], o_raw[:, :], ALU.add).then_inc(s["x1_set"], 1)

            def back_norm(u):
                rsqrt(u + 1, b_rstd[:, :], "b_rstd_set", b_var[:, :], "b_var_set", b_mv[:, 1:2], "b_mv_set",
                      1, ln_eps)

            def back_rope(u):
                pool.wait_ge(s["qk_set"], u + 1)
                g.tensor_tensor(r_a[:, :], qk[:, :], rope_a[:, :], ALU.mult).then_inc(s["r_ab_set"], 1)
                g.tensor_tensor(r_b[:, :], qk[:, :], rope_b[:, :], ALU.mult).then_inc(s["r_ab_set"], 1)
                rsqrt(u + 1, sq_rinv[:, :], "sq_rinv_set", sq_mean[:, :], "sq_mean_set", sq[:, :], "sq_set",
                      2, rms_eps, 2)
                pool.wait_ge(s["v_set"], u + 1)
                g.tensor_tensor(v_of[:, :, :], v[:, :].unsqueeze(1).to_broadcast([P, TB, D]),
                                of_batch.unsqueeze(2).to_broadcast([P, TB, D]), ALU.mult).then_inc(s["v_of_set"], 1)

            def back_y(u):
                rsqrt(u + 1, y_rinv[:, :], "y_rinv_set", y_mean[:, :], "y_mean_set", y_sq[:, :], "y_sq_set",
                      1, rms_eps)

            def back_f(u):
                rsqrt(u + 1, f_rstd[:, :], "f_rstd_set", f_var[:, :], "f_var_set", f_mv[:, 1:2], "f_mv_set",
                      1, ln_eps)
                pool.wait_ge(s["x2_set"], u + 1)
                g.tensor_tensor(x2_b[:, :], x2[:, :], fbias[:, :], ALU.add).then_inc(s["x2_b_set"], 1)

            def step(t, front, back):
                u = t - 1
                n = STEP * t + FRONT
                if front:
                    norm_front(t + 1)
                    n = n + FRONT
                if back:
                    back_norm(u)
                    back_rope(u)
                    back_y(u)
                    back_f(u)
                add_mix9(t, n + J_MIX)
                residual(t, n + J_MIX + J_V + J_O)

            g.memset(minus_half[:, :], -0.5).then_inc(s["half_set"], 1)
            g.memset(ln_eps[:, :], LN_EPS).then_inc(s["half_set"], 1)
            g.memset(rms_eps[:, :], RMS_EPS * D).then_inc(s["half_set"], 1)
            pool.wait_ge(s["half_set"], 3)
            norm_front(0)
            pool.wait_ge(s["ln_rstd_set"], 1)
            g.memset(wk[64:128, 0:H:2, :], 0.0).then_inc(s["zeros_set"], 1)
            pool.wait_ge(s["zeros_set"], 1)
            g.memset(wk[0:64, 1:H:2, :], 0.0).then_inc(s["zeros_set"], 1)
            pool.wait_ge(s["zeros_set"], 2)
            g.memset(keys_t[:, :, :, NKV:KEYS], 0.0).then_inc(s["pads_set"], 1)
            pool.wait_ge(s["self_in"], 16 * 7)
            pool.wait_ge(s["const_in"], 16)
            pool.wait_ge(s["ffn_in"], 64)
            pool.wait_ge(s["x0_in"], 16)
            pool.wait_ge(s["x_in"], 16)
            for i in range(2):
                half = slice(i * D, (i + 1) * D)
                g.tensor_tensor(rope_a[:, half], gains[:, half], const[:, C_COS:C_COS + D], ALU.mult)\
                    .then_inc(s["rope_set"], 1)
                g.tensor_tensor(rope_b[:, half], gains[:, half], const[:, C_SIN:C_SIN + D], ALU.mult)\
                    .then_inc(s["rope_set"], 1)
            g.tensor_tensor(gout[:, :], gout[:, :], const[:, C_ROOT:C_ROOT + 1].to_broadcast([P, D]), ALU.mult)\
                .then_inc(s["rope_set"], 1)
            step(0, True, False)
            pool.wait_ge(s["rope_set"], 5)
            with pool.Fori(1, TILES - 1) as t:
                step(t, True, True)
            step(TILES - 1, False, True)
            for stage in (back_norm, back_rope, back_y, back_f):
                stage(TILES - 1)


def kernel(x, ctx_1024, L0_xattn_Wq, L0_xattn_Wkv, L0_xattn_Wout, L0_xattn_bout, L0_attn_Wqkv, L0_attn_bqkv,
           L0_attn_gq, L0_attn_gk, L0_attn_Wout, L0_attn_bout, L0_attn_gout, L0_ffn_packed_weight,
           L0_ffn_weight_scale, L0_ffn_bias):
    import concourse.bacc as _bacc
    from concourse.bass_utils import run_bass_kernel_spmd as _run

    c = np.asarray(ctx_1024).reshape(TILES, TB, NKV, D)
    wkv = np.asarray(L0_xattn_Wkv)
    by_group = c[:, :, :NKV - 1, :].reshape(TILES, TB, M - 1, 2, 2, GQ, D).transpose(0, 4, 2, 5, 1, 3, 6)
    arrays = {
        "x": np.asarray(x).reshape(BATCH * NQ, D),
        "ctx_t": c.reshape(TILES, TB, NKV, KD, P).transpose(0, 4, 3, 1, 2).reshape(TILES, P, KD * TB, NKV),
        "ctx_k": by_group.reshape(TILES, P, TB, 2, D),
        "ctx_9": c[:, :, NKV - 1, :],
        "const": constants(),
        "wq": L0_xattn_Wq, "wk_t": wkv[:, :INNER].T, "wv": wkv[:, INNER:], "wo": L0_xattn_Wout, "bo": L0_xattn_bout,
        "swqkv_t": np.asarray(L0_attn_Wqkv).T, "sbqkv": L0_attn_bqkv, "sgq": L0_attn_gq, "sgk": L0_attn_gk,
        "swo_t": np.asarray(L0_attn_Wout).T, "sbo": L0_attn_bout, "sgout": L0_attn_gout,
        "packed_t": np.asarray(L0_ffn_packed_weight).reshape(64, D).T,
        "wscale": L0_ffn_weight_scale, "fbias": L0_ffn_bias,
    }
    nc = _bacc.Bacc("TRN2", target_bir_lowering=False, num_devices=1)
    ins, given = {}, {}
    for name, v in arrays.items():
        v = np.ascontiguousarray(v)
        given[f"in_{name}"] = v
        ins[name] = nc.dram_tensor(f"in_{name}", v.shape, mybir.dt.from_np(v.dtype), kind="ExternalInput").ap()
    out = nc.dram_tensor("out", (TILES, P, D), F32, kind="ExternalOutput").ap()
    build(nc, ins, out)
    r = _run(nc, [given], core_ids=[0])
    return r.results[0]["out"].reshape(BATCH, NQ, D)
```

```python
from contextlib import ExitStack

import numpy as np

import concourse.bass as bass
from concourse import mybir

P = 128
D = 256
KD = D // P
BATCH, NQ, NKV = 32, 32, 257
TILES = BATCH * NQ // P
TB = P // NQ
H, DH = 16, 64
INNER = H * DH
HP = H // 2
GQ = 8
G = NQ // GQ
M = NKV // NQ + 1
MR = M * GQ
KEYS = M * NQ
SH, SD = 16, 16
HH = SH // KD
KVW = P + HH
SCALE = float(DH) ** -0.5
LN_EPS, RMS_EPS, LIN_EPS = 1e-5, 1.1920929e-07, 1e-6
NEG = -1e30
ROUND = float(3 << 22)

F32 = mybir.dt.float32
BF16 = mybir.dt.bfloat16
I32 = mybir.dt.int32
ALU = mybir.AluOpType
ACT = mybir.ActivationFunctionType
X = mybir.AxisListType.X

RING = 3
J_Q, J_QT, J_MIX, J_V, J_O = 2, 8, 8, 2, 1
FRONT = J_Q + J_QT
STEP = FRONT + J_MIX + J_V + J_O
assert STEP % RING == 0

C_ID = 0
C_BD = C_ID + P
C_COS = C_BD + P
C_SIN = C_COS + D
C_EYE = C_SIN + D
C_ABSENT = C_EYE + GQ
C_B = C_ABSENT + G * M
C_H = C_B + TB
C_ROOT = C_H + HH
C_W = C_ROOT + 1


def mix_part(j):
    return j // 2 % 2, j % 2, j // 4


def constants():
    c = np.zeros((P, C_W), np.float32)
    p = np.arange(P)
    c[:, C_ID:C_ID + P] = np.eye(P)
    c[:, C_BD:C_BD + P] = p[:, None] // SD == p[None, :] // SD
    freq = 1.0 / 10000.0 ** (np.arange(0, SD, 2) / SD)
    angle = np.repeat((p % NQ)[:, None] * freq[None, :], 2, axis=1)
    sign = np.where(np.arange(SD) % 2 == 0, 1.0, -1.0)
    root = float(D) ** 0.5
    c[:, C_COS:C_COS + D] = np.tile(np.cos(angle) * root, (1, SH))
    c[:, C_SIN:C_SIN + D] = np.tile(np.sin(angle) * sign * root, (1, SH))
    c[:, C_ROOT] = root
    c[:, C_EYE:C_EYE + GQ] = p[:, None] % GQ == np.arange(GQ)[None, :]
    absent = np.zeros((P, G, M), np.float32)
    absent[:, :, M - 1] = NEG
    absent[p % GQ == 0, 0, M - 1] = 0.0
    c[:, C_ABSENT:C_ABSENT + G * M] = absent.reshape(P, G * M)
    c[:, C_B:C_B + TB] = p[:, None] // NQ == np.arange(TB)[None, :]
    c[:, C_H:C_H + HH] = p[:, None] // SD == np.arange(HH)[None, :]
    return c


def build(nc, a, out):
    with ExitStack() as ctx:
        def sb(name, shape, dt=F32):
            return ctx.enter_context(nc.sbuf_tensor(name, shape, dt))

        def ps(name):
            return ctx.enter_context(nc.psum_tensor(name, [P, 512], F32))

        def sem(name):
            return ctx.enter_context(nc.semaphore(name))

        const = sb("const", [P, C_W])
        ident = const[:, C_ID:C_ID + P]
        same_head = const[:, C_BD:C_BD + P]
        eye8 = const[:, C_EYE:C_EYE + GQ]
        absent = const[:, C_ABSENT:C_ABSENT + G * M]
        of_batch = const[:, C_B:C_B + TB]
        of_head = const[:, C_H:C_H + HH]
        ident16 = sb("ident16", [P, P], BF16)
        wq = sb("wq", [P, KD, INNER])
        wk = sb("wk", [P, H, D])
        wv = sb("wv", [P, KD, INNER])
        wo = sb("wo", [P, HP, D])
        bo = sb("bo", [P, D])
        sw = sb("sw", [P, KD, 3 * D])
        sbias = sb("sbias", [P, 3 * D])
        gains = sb("gains", [P, 2 * D])
        rope_a = sb("rope_a", [P, 2 * D])
        rope_b = sb("rope_b", [P, 2 * D])
        swo = sb("swo", [P, KD, D])
        sbo = sb("sbo", [P, D])
        gout = sb("gout", [P, D])
        packed = sb("packed", [P, KD, 64], I32)
        codes = sb("codes", [P, KD, 4, 64], I32)
        fw = sb("fw", [P, KD, D], BF16)
        wscale = sb("wscale", [P, 1])
        fbias = sb("fbias", [P, D])
        minus_half = sb("minus_half", [P, 2])
        ln_eps = sb("ln_eps", [P, 2])
        rms_eps = sb("rms_eps", [P, 2])

        x_all = sb("x_all", [P, TILES, D])
        keys_t = sb("keys_t", [P, KD, TB, KEYS])
        keys = sb("keys", [P, TB, 2, D])
        key9 = sb("key9", [TB, D])
        ln_stats = sb("ln_stats", [P, 6])
        ln_mv = sb("ln_mv", [P, 2])
        ln_var = sb("ln_var", [P, 1])
        ln_rstd = sb("ln_rstd", [P, 1])
        xn = sb("xn", [P, D])
        xn_t = sb("xn_t", [P, KD, P])
        q_t = sb("q_t", [P, HP, P])
        qt = sb("qt", [P, KD, TB * G, H, GQ])
        masked = sb("masked", [P, 2, G * M, GQ])
        sc = sb("sc", [P, TB * G, M])
        sc_max = sb("sc_max", [P, TB * G])
        sc_off = sb("sc_off", [P, TB * G, M])
        expd = sb("expd", [P, TB * G, M])
        sc_sum = sb("sc_sum", [P, TB * G])
        sc_inv = sb("sc_inv", [P, TB * G])
        prob = sb("prob", [P, TB * G, M])
        spread = sb("spread", [P, TB * G, M - 1, GQ])
        prob9 = sb("prob9", [TB, TB, H])
        prob_t = sb("prob_t", [P, 2 * TB, P])
        mix9 = sb("mix9", [P, KD, TB, H])
        mix = sb("mix", [P, KD, TB, G, H, GQ])
        att_t = sb("att_t", [P, HP, P])
        o_raw = sb("o_raw", [P, D])
        x_bo = sb("x_bo", [P, D])

        x1 = sb("x1", [P, D])
        b_stats = sb("b_stats", [P, 6])
        b_mv = sb("b_mv", [P, 2])
        b_var = sb("b_var", [P, 1])
        b_rstd = sb("b_rstd", [P, 1])
        b_xn = sb("b_xn", [P, D])
        b_xn_t = sb("b_xn_t", [P, KD, P])
        qk = sb("qk", [P, 2 * D])
        v = sb("v", [P, D])
        junk = sb("junk", [P, D])
        sq = sb("sq", [P, 2])
        sq_mean = sb("sq_mean", [P, 2])
        sq_rinv = sb("sq_rinv", [P, 2])
        r_a = sb("r_a", [P, 2 * D])
        r_b = sb("r_b", [P, 2 * D])
        roped = sb("roped", [P, 2 * D])
        feat = sb("feat", [P, 2 * D])
        v_of = sb("v_of", [P, TB, D])
        qf_t = sb("qf_t", [P, KD, P])
        state = sb("state", [P, KD, TB, KVW])
        den = sb("den", [P, KD, HH])
        den_inv = sb("den_inv", [P, KD, HH])
        lin = sb("lin", [P, D])
        lin_t = sb("lin_t", [P, KD, P])
        y = sb("y", [P, D])
        junk_y = sb("junk_y", [P, D])
        y_sq = sb("y_sq", [P, 1])
        y_mean = sb("y_mean", [P, 1])
        y_rinv = sb("y_rinv", [P, 1])
        y_g = sb("y_g", [P, D])
        x2 = sb("x2", [P, D])
        x2_b = sb("x2_b", [P, D])
        f_stats = sb("f_stats", [P, 6])
        f_mv = sb("f_mv", [P, 2])
        f_var = sb("f_var", [P, 1])
        f_rstd = sb("f_rstd", [P, 1])
        f_xn = sb("f_xn", [P, D])
        amax = sb("amax", [P, 1])
        amax_g = sb("amax_g", [P, 1])
        act_inv = sb("act_inv", [P, 1])
        act_scale = sb("act_scale", [P, 1])
        dq = sb("dq", [P, 1])
        dq_w = sb("dq_w", [P, 1])
        f_q = sb("f_q", [P, D])
        f_r = sb("f_r", [P, D])
        f_i = sb("f_i", [P, D], BF16)
        f_t = sb("f_t", [P, KD, P], BF16)
        x3 = sb("x3", [P, D])

        ring = [ps(f"ring{i}") for i in range(RING)]
        ps_s = [ps(f"ps_s{i}") for i in range(2)]
        ps_x, ps_y, ps_z = ps("ps_x"), ps("ps_y"), ps("ps_z")

        names = """x0_in x_in ident_in const_in wq0_in wq1_in wk_in wv_in wo_in bo_in self_in ffn_in keys_t_in keys_in
            zeros_set pads_set half_set ident16_set rope_set codes_set fw_set
            ln_stats_first ln_stats_set ln_mv_set ln_var_set ln_rstd_set xn_set xn_t_filled xn_t_set
            ring_filled ring_drained
            scores_filled masked_set scores_drained sc_set sc_added max_set off_set exp_set sum_set inv_set prob_set spread_set
            prob9_filled prob9_set prob_t_filled prob_t_set mix9_filled mix9_set mix_set x_bo_set x1_set
            b_stats_first b_stats_set b_mv_set b_var_set b_rstd_set b_xn_set b_xn_t_filled b_xn_t_set
            qk_filled v_filled qk_set v_set sq_set sq_mean_set sq_rinv_set r_a_set r_b_set roped_set feat_set v_of_set
            kv_filled qf_t_set state_set num_filled den_set den_inv_set lin_set lin_t_filled lin_t_set
            y_filled y_set y_sq_set y_mean_set y_rinv_set y_g_set x2_set x2_b_set
            f_stats_set f_mv_set f_var_set f_rstd_set f_xn_set amax_set amax_g_set act_inv_set act_scale_set
            dq_set dq_w_set f_q_set f_r_set f_i_set f_t_filled f_t_set f_filled x3_set out_stored""".split()
        s = {n: sem(n) for n in names}

        block = ctx.enter_context(nc.Block())

        @block.sync
        def _(sp):
            def load_keys_t(t):
                sp.dma_start(keys_t[:, :, :, 0:NKV].rearrange("p k b j -> p (k b) j"),
                             a["ctx_t"][t]).then_inc(s["keys_t_in"], 16)

            def load_keys(t):
                sp.dma_start(keys[:, :, :, :], a["ctx_k"][t]).then_inc(s["keys_in"], 16)
                sp.dma_start(key9[:, :], a["ctx_9"][t]).then_inc(s["keys_in"], 16)

            def broadcast(o, name, w, done):
                sp.dma_start(o, a[name].rearrange("(o n) -> o n", o=1).to_broadcast([P, w])).then_inc(s[done], 16)

            x_v = a["x"].rearrange("(t p) d -> p t d", p=P)
            wq_v = a["wq"].rearrange("(k p) n -> p k n", p=P)
            sp.dma_start(x_all[:, 0, :], x_v[:, 0, :]).then_inc(s["x0_in"], 16)
            sp.dma_start(const[:, 0:P], a["const"][:, 0:P]).then_inc(s["ident_in"], 16)
            for j in range(J_Q):
                cols = slice(j * INNER // J_Q, (j + 1) * INNER // J_Q)
                sp.dma_start(wq[:, :, cols], wq_v[:, :, cols]).then_inc(s[f"wq{j}_in"], 16)
            for half in range(2):
                rows = slice(half * DH, (half + 1) * DH)
                sp.dma_start(wk[rows, half:H:2, :],
                             a["wk_t"].rearrange("(c r) d -> r c d", r=P)[rows, :, :]).then_inc(s["wk_in"], 16)
            sp.dma_start(const[:, P:C_W], a["const"][:, P:C_W]).then_inc(s["const_in"], 16)
            load_keys_t(0)
            sp.dma_start(x_all[:, 1:TILES, :], x_v[:, 1:TILES, :]).then_inc(s["x_in"], 16)
            load_keys(0)
            broadcast(bo[:, :], "bo", D, "bo_in")
            sp.dma_start(wv[:, :, :], a["wv"].rearrange("(k p) n -> p k n", p=P)).then_inc(s["wv_in"], 16)
            sp.dma_start(wo[:, :, :], a["wo"].rearrange("(c p) n -> p c n", p=P)).then_inc(s["wo_in"], 16)
            broadcast(gains[:, 0:D], "sgq", D, "self_in")
            broadcast(gains[:, D:2 * D], "sgk", D, "self_in")
            broadcast(gout[:, :], "sgout", D, "self_in")
            sp.dma_start(sw[:, :, :], a["swqkv_t"].rearrange("(k p) n -> p k n", p=P)).then_inc(s["self_in"], 16)
            sp.dma_start(swo[:, :, :], a["swo_t"].rearrange("(k p) n -> p k n", p=P)).then_inc(s["self_in"], 16)
            broadcast(sbias[:, :], "sbqkv", 3 * D, "self_in")
            broadcast(sbo[:, :], "sbo", D, "self_in")
            broadcast(fbias[:, :], "fbias", D, "ffn_in")
            broadcast(wscale[:, :], "wscale", 1, "ffn_in")
            sp.dma_start(packed[:, :, :], a["packed_t"].rearrange("(k p) n -> p k n", p=P)).then_inc(s["ffn_in"], 16)

            def stores(t):
                sp.wait_ge(s["x3_set"], t + 1)
                sp.dma_start(out[t], x3[:, :]).then_inc(s["out_stored"], 16)

            def step(t, back):
                sp.wait_ge(s["scores_filled"], TB * t + TB)
                load_keys_t(t + 1)
                sp.wait_ge(s["ring_filled"], STEP * t + FRONT + FRONT + J_MIX)
                load_keys(t + 1)
                if back:
                    stores(t - 1)

            step(0, False)
            with sp.Fori(1, TILES - 1) as t:
                step(t, True)
            stores(TILES - 2)
            stores(TILES - 1)
            sp.wait_ge(s["out_stored"], 16 * TILES)

        @block.tensor
        def _(pe):
            mm = nc.tensor.matmul

            def ring_job(n, phase, c):
                if isinstance(n, int) and n + c < RING:
                    return ring[(phase + c) % RING]
                pe.wait_ge(s["ring_drained"], n + (c - RING + 1))
                return ring[(phase + c) % RING]

            def transpose_xn(t, first=False):
                pe.wait_ge(s["xn_set"], t + 1)
                for k in range(KD):
                    last = nc.tensor.transpose(ps_z[:, k * P:(k + 1) * P], xn[:, k * P:(k + 1) * P], ident)
                last.then_inc(s["xn_t_filled"], 1)

            def q_jobs(t, n, phase):
                pe.wait_ge(s["xn_t_set"], t + 1)
                for j in range(J_Q):
                    if isinstance(t, int) and t == 0:
                        pe.wait_ge(s[f"wq{j}_in"], 16)
                    bank = ring_job(n, phase, j)
                    for c in range(4):
                        hp = 4 * j + c
                        for k in range(KD):
                            last = mm(bank[:, c * P:(c + 1) * P], wq[:, k, hp * P:(hp + 1) * P], xn_t[:, k, :],
                                      start=(k == 0), stop=(k == KD - 1))
                    last.then_inc(s["ring_filled"], 1)

            def qt_jobs(n, phase, jobs):
                for j in jobs:
                    heads, k = j // KD, j % KD
                    bank = ring_job(n, phase, J_Q + j)
                    pe.wait_ge(s["ring_drained"], n + 1 + (4 * heads + 3) // 8)
                    for c in range(4):
                        h = 4 * heads + c
                        last = mm(bank[:, c * P:(c + 1) * P], wk[:, h, k * P:(k + 1) * P], q_t[:, h // 2, :],
                                  start=True, stop=True)
                    last.then_inc(s["ring_filled"], 1)

            def scores(t, batches):
                for b in batches:
                    if b == 0:
                        pe.wait_ge(s["keys_t_in"], 16 * t + 16)
                    if b >= 2:
                        pe.wait_ge(s["scores_drained"], TB * t + b - 1)
                    elif not (isinstance(t, int) and t == 0):
                        pe.wait_ge(s["prob_t_set"], 2 * t + b - 1)
                    for g in range(G):
                        for k in range(KD):
                            last = mm(ps_s[b % 2][:, g * MR:(g + 1) * MR],
                                      qt[:, k, b * G + g, :, :].rearrange("p h q -> p (h q)"),
                                      keys_t[:, k, b, :].rearrange("p (m q) -> p m q", m=M)[:, :, g * GQ:(g + 1) * GQ],
                                      start=(k == 0), stop=(k == KD - 1))
                    last.then_inc(s["scores_filled"], 1)

            def transpose_prob(t):
                if not (isinstance(t, int) and t == 0):
                    pe.wait_ge(s["b_xn_t_set"], t)
                pe.wait_ge(s["prob_set"], t + 1)
                mm(ps_z[0:TB, 0:H], prob[:, 0:TB * G:G, M - 1], ident[:, 0:P:GQ], start=True, stop=True)\
                    .then_inc(s["prob9_filled"], 1)
                for j in range(2):
                    pe.wait_ge(s["spread_set"], 2 * t + j + 1)
                    pe.wait_ge(s["scores_drained"], TB * t + 3 + j)
                    for c in range(4):
                        pair = 4 * j + c
                        last = nc.tensor.transpose(ps_s[j][:, c * P:(c + 1) * P],
                                                   spread[:, 2 * pair:2 * pair + 2, :, :].rearrange("p g m r -> p (g m r)"),
                                                   ident)
                    last.then_inc(s["prob_t_filled"], 1)

            def mix9_job(t):
                pe.wait_ge(s["prob9_set"], t + 1)
                pe.wait_ge(s["keys_in"], 32 * t + 32)
                for k in range(KD):
                    last = mm(ps_z[:, k * TB * H:(k + 1) * TB * H], key9[:, k * P:(k + 1) * P],
                              prob9[:, :, :], start=True, stop=True)
                last.then_inc(s["mix9_filled"], 1)

            def mix_jobs(t, n, phase, jobs):
                for j in jobs:
                    b2, k, half = mix_part(j)
                    rows = slice(half * 64, half * 64 + 64)
                    bank = ring_job(n, phase, j)
                    pe.wait_ge(s["prob_t_set"], 2 * t + 1 + b2)
                    for c in range(4):
                        b, g2 = 2 * b2 + c // 2, c % 2
                        last = mm(bank[:, c * P:(c + 1) * P], keys[rows, b, g2, k * P:(k + 1) * P],
                                  prob_t[rows, 2 * b + g2, :], start=True, stop=True)
                    last.then_inc(s["ring_filled"], 1)

            def value_jobs(t, n, phase):
                pe.wait_ge(s["mix_set"], t + 1)
                pe.wait_ge(s["ring_drained"], n)
                if isinstance(t, int) and t == 0:
                    pe.wait_ge(s["wv_in"], 16)
                    pe.wait_ge(s["wo_in"], 16)
                for j in range(J_V):
                    bank = ring_job(n, phase, j)
                    for c in range(4):
                        for k in range(KD):
                            for half in range(2):
                                h = 2 * (4 * j + c) + half
                                last = mm(bank[half * DH:(half + 1) * DH, c * P:(c + 1) * P],
                                          wv[:, k, h * DH:(h + 1) * DH],
                                          mix[:, k, :, :, h, :].rearrange("p b g q -> p (b g) q"),
                                          start=(k == 0), stop=(k == KD - 1), skip_group_check=True)
                    last.then_inc(s["ring_filled"], 1)

            def out_job(n, phase, part):
                pe.wait_ge(s["ring_drained"], n - J_V + 1 + part)
                for c in range(4 * part, 4 * part + 4):
                    last = mm(ring[phase % RING][:, 0:D], att_t[:, c, :], wo[:, c, :],
                              start=(c == 0), stop=(c == HP - 1))
                if part:
                    last.then_inc(s["ring_filled"], 1)

            def back_xn(u):
                pe.wait_ge(s["b_xn_set"], u + 1)
                for k in range(KD):
                    last = nc.tensor.transpose(ps_z[:, k * P:(k + 1) * P], b_xn[:, k * P:(k + 1) * P], ident)
                last.then_inc(s["b_xn_t_filled"], 1)

            def back_qkv(u):
                pe.wait_ge(s["b_xn_t_set"], u + 1)
                for bank, at, width, filled in ((ps_x, 0, 2 * D, "qk_filled"), (ps_y, 2 * D, D, "v_filled")):
                    for k in range(KD):
                        last = mm(bank[:, 0:width], b_xn_t[:, k, :], sw[:, k, at:at + width],
                                  start=(k == 0), stop=(k == KD - 1))
                    last.then_inc(s[filled], 1)

            def back_kv(u, more=True):
                pe.wait_ge(s["mix9_set"], u + 2 if more else u + 1)
                pe.wait_ge(s["feat_set"], 2 * u + 2)
                pe.wait_ge(s["v_of_set"], u + 1)
                for k in range(KD):
                    nc.tensor.transpose(ps_z[:, k * P:(k + 1) * P], feat[:, k * P:(k + 1) * P], ident)
                    kf = feat[:, D + k * P:D + (k + 1) * P]
                    mm((ps_x, ps_y)[k][:, :], kf, v_of[:, :, k * P:(k + 1) * P], start=True, stop=True)
                    last = mm(ps_z[:, D + k * TB:D + (k + 1) * TB], kf, of_batch, start=True, stop=True)
                last.then_inc(s["kv_filled"], 1)

            def back_num(u):
                pe.wait_ge(s["qf_t_set"], u + 1)
                pe.wait_ge(s["state_set"], 4 * u + 4)
                for k in range(KD):
                    for b in range(TB):
                        last = mm(ps_x[b * NQ:(b + 1) * NQ, k * KVW:(k + 1) * KVW], qf_t[:, k, b * NQ:(b + 1) * NQ],
                                  state[:, k, b, :], start=True, stop=True)
                last.then_inc(s["num_filled"], 1)

            def back_lin(u):
                pe.wait_ge(s["lin_set"], u + 1)
                for k in range(KD):
                    last = nc.tensor.transpose(ps_z[:, k * P:(k + 1) * P], lin[:, k * P:(k + 1) * P], ident)
                last.then_inc(s["lin_t_filled"], 1)

            def back_out(u):
                pe.wait_ge(s["lin_t_set"], u + 1)
                for k in range(KD):
                    last = mm(ps_y[:, 0:D], lin_t[:, k, :], swo[:, k, :], start=(k == 0), stop=(k == KD - 1))
                last.then_inc(s["y_filled"], 1)

            def back_quant(u):
                pe.wait_ge(s["f_i_set"], u + 1)
                for k in range(KD):
                    last = nc.tensor.transpose(ps_z[:, k * 64:(k + 1) * 64].bitcast(BF16),
                                               f_i[:, k * P:(k + 1) * P], ident16[:, :])
                last.then_inc(s["f_t_filled"], 1)

            def back_ffn(u):
                pe.wait_ge(s["f_t_set"], u + 1)
                for k in range(KD):
                    last = mm(ps_x[:, 0:D], f_t[:, k, :], fw[:, k, :], start=(k == 0), stop=(k == KD - 1))
                last.then_inc(s["f_filled"], 1)

            def step(t, front, back):
                u = t - 1
                n, phase = STEP * t + FRONT, FRONT
                scores(t, (0, 1))
                if front:
                    transpose_xn(t + 1)
                scores(t, (2,))
                if back:
                    if front:
                        pe.wait_ge(s["xn_t_set"], t + 2)
                    back_xn(u)
                if front:
                    scores(t, (3,))
                    q_jobs(t + 1, n, phase)
                    if back:
                        back_qkv(u)
                    qt_jobs(n, phase, range(0, 4))
                    if not back:
                        pe.wait_ge(s["xn_t_set"], t + 2)
                    transpose_prob(t)
                    qt_jobs(n, phase, range(4, 6))
                    mix9_job(t)
                    qt_jobs(n, phase, range(6, J_QT))
                    n, phase = n + FRONT, phase + FRONT
                    if back:
                        back_kv(u)
                    mix_jobs(t, n, phase, range(0, 3))
                else:
                    scores(t, (3,))
                    back_qkv(u)
                    transpose_prob(t)
                    mix9_job(t)
                    mix_jobs(t, n, phase, range(0, 2))
                    back_kv(u)
                    mix_jobs(t, n, phase, range(2, 3))
                if back:
                    back_num(u)
                mix_jobs(t, n, phase, range(3, 5))
                if back:
                    back_lin(u)
                mix_jobs(t, n, phase, range(5, J_MIX))
                if back:
                    back_out(u)
                value_jobs(t, n + J_MIX, phase + J_MIX)
                out_job(n + J_MIX + J_V, phase + J_MIX + J_V, 0)
                if back:
                    back_quant(u)
                out_job(n + J_MIX + J_V, phase + J_MIX + J_V, 1)
                if back:
                    back_ffn(u)

            pe.wait_ge(s["ident_in"], 16)
            transpose_xn(0)
            q_jobs(0, 0, 0)
            pe.wait_ge(s["wk_in"], 32)
            pe.wait_ge(s["zeros_set"], 2)
            qt_jobs(0, 0, range(J_QT))
            pe.wait_ge(s["ring_drained"], FRONT)
            pe.wait_ge(s["pads_set"], 1)
            pe.wait_ge(s["const_in"], 16)
            step(0, True, False)
            pe.wait_ge(s["self_in"], 16 * 7)
            pe.wait_ge(s["ident16_set"], 1)
            pe.wait_ge(s["fw_set"], 1)
            with pe.Fori(1, TILES - 1) as t:
                step(t, True, True)
            step(TILES - 1, False, True)
            u = TILES - 1
            back_xn(u)
            back_qkv(u)
            back_kv(u, more=False)
            back_num(u)
            back_lin(u)
            back_out(u)
            back_quant(u)
            back_ffn(u)

        @block.scalar
        def _(act):
            def copy(o, i):
                return nc.scalar.activation(o, i, ACT.Copy)

            def drain(n, c, o, i):
                act.wait_ge(s["ring_filled"], n + (c + 1))
                copy(o, i).then_inc(s["ring_drained"], 1)

            def drain_xn(t):
                act.wait_ge(s["xn_t_filled"], t + 1)
                copy(xn_t[:, :, :], ps_z[:, 0:D]).then_inc(s["xn_t_set"], 1)

            def drain_q(n, phase):
                for j in range(J_Q):
                    drain(n, j, q_t[:, 4 * j:4 * j + 4, :], ring[(phase + j) % RING][:, :])

            def drain_qt(n, phase, jobs):
                for j in jobs:
                    heads, k = j // KD, j % KD
                    drain(n, J_Q + j, qt[:, k, :, 4 * heads:4 * heads + 4, :].rearrange("p g h q -> p h g q"),
                          ring[(phase + J_Q + j) % RING][:, :].rearrange("p (h g q) -> p h g q", h=4, q=GQ))

            def exponentials(t):
                act.wait_ge(s["off_set"], t + 1)
                nc.scalar.activation(expd[:, :, :], sc_off[:, :, :], ACT.Exp, scale=SCALE).then_inc(s["exp_set"], 1)

            def drain_mix(n, phase, jobs):
                for j in jobs:
                    b2, k, half = mix_part(j)
                    drain(n, j, mix[:, k, 2 * b2:2 * b2 + 2, half:G:2, :, :].rearrange("p b g h q -> p b g (h q)"),
                          ring[(phase + j) % RING][:, :].rearrange("p (b g n) -> p b g n", b=2, g=2))

            def drain_values(n, phase):
                for j in range(J_V):
                    drain(n, j, att_t[:, 4 * j:4 * j + 4, :], ring[(phase + j) % RING][:, :])

            def drain_mix9(t):
                act.wait_ge(s["mix9_filled"], t + 1)
                copy(mix9[:, :, :, :], ps_z[:, 0:KD * TB * H]).then_inc(s["mix9_set"], 1)

            def back_xn(u):
                act.wait_ge(s["b_xn_t_filled"], u + 1)
                copy(b_xn_t[:, :, :], ps_z[:, 0:D]).then_inc(s["b_xn_t_set"], 1)

            def back_squares(u):
                act.wait_ge(s["qk_set"], u + 1)
                for i in range(2):
                    if i:
                        act.wait_ge(s["sq_set"], 2 * u + 1)
                    elif not (isinstance(u, int) and u == 0):
                        act.wait_ge(s["sq_set"], 2 * u)
                    nc.scalar.activation(junk[:, :], qk[:, i * D:(i + 1) * D], ACT.Square,
                                         accum_out=sq[:, i:i + 1]).then_inc(s["sq_set"], 1)

            def back_qf(u):
                act.wait_ge(s["kv_filled"], u + 1)
                copy(qf_t[:, :, :], ps_z[:, 0:D]).then_inc(s["qf_t_set"], 1)

            def back_lin(u):
                act.wait_ge(s["lin_t_filled"], u + 1)
                copy(lin_t[:, :, :], ps_z[:, 0:D]).then_inc(s["lin_t_set"], 1)

            def back_y(u):
                act.wait_ge(s["y_set"], u + 1)
                nc.scalar.activation(junk_y[:, :], y[:, :], ACT.Square, accum_out=y_sq[:, :]).then_inc(s["y_sq_set"], 1)

            def back_quant(u):
                act.wait_ge(s["f_t_filled"], u + 1)
                copy(f_t[:, :, :], ps_z[:, 0:P].bitcast(BF16)).then_inc(s["f_t_set"], 1)

            def step(t, front, back):
                u = t - 1
                n, phase = STEP * t + FRONT, FRONT
                if front:
                    drain_xn(t + 1)
                if back:
                    back_xn(u)
                if front:
                    drain_q(n, phase)
                exponentials(t)
                if front:
                    drain_qt(n, phase, range(0, 1))
                    if back:
                        back_squares(u)
                    drain_qt(n, phase, range(1, 5))
                    drain_qt(n, phase, range(5, 6))
                    drain_mix9(t)
                    drain_qt(n, phase, range(6, J_QT))
                    n, phase = n + FRONT, phase + FRONT
                    if back:
                        back_qf(u)
                    drain_mix(n, phase, range(0, 3))
                else:
                    back_squares(u)
                    drain_mix9(t)
                    drain_mix(n, phase, range(0, 1))
                    drain_mix(n, phase, range(1, 2))
                    back_qf(u)
                    drain_mix(n, phase, range(2, 3))
                drain_mix(n, phase, range(3, 5))
                if back:
                    back_lin(u)
                drain_mix(n, phase, range(5, J_MIX))
                if back:
                    back_y(u)
                drain_values(n + J_MIX, phase + J_MIX)
                if back:
                    back_quant(u)
                drain(n + J_MIX + J_V, 0, o_raw[:, :], ring[(phase + J_MIX + J_V) % RING][:, 0:D])

            drain_xn(0)
            drain_q(0, 0)
            drain_qt(0, 0, range(J_QT))
            step(0, True, False)
            with act.Fori(1, TILES - 1) as t:
                step(t, True, True)
            step(TILES - 1, False, True)
            u = TILES - 1
            for stage in (back_xn, back_squares, back_qf, back_lin, back_y, back_quant):
                stage(u)

        @block.vector
        def _(dve):
            V = nc.vector

            def moments(src, stats, stats_s, count, mv, mv_s):
                V.bn_stats(stats[:, :], src).then_inc(s[stats_s], 1)
                dve.wait_ge(s[stats_s], 1)
                dve.wait_ge(s[stats_s], count)
                V.bn_aggr(mv[:, :], stats[:, :]).then_inc(s[mv_s], 1)

            def normalise(t1, src, mv, rstd, rstd_s, o, o_s):
                dve.wait_ge(s[rstd_s], t1)
                V.tensor_scalar(o, src, mv[:, 0:1], rstd[:, 0:1], ALU.subtract, ALU.mult).then_inc(s[o_s], 1)

            def front_moments(t):
                stats_s, count = ("ln_stats_first", t + 1) if isinstance(t, int) else ("ln_stats_set", t - 1)
                moments(x_all[:, t, :], ln_stats, stats_s, count, ln_mv, "ln_mv_set")

            def front_norm(t):
                if not (isinstance(t, int) and t == 0):
                    dve.wait_ge(s["xn_t_filled"], t)
                normalise(t + 1, x_all[:, t, :], ln_mv, ln_rstd, "ln_rstd_set", xn[:, :], "xn_set")

            def take_scores(t, batches):
                for b in batches:
                    dve.wait_ge(s["scores_filled"], TB * t + b + 1)
                    V.tensor_tensor(masked[:, b % 2, :, :],
                                    ps_s[b % 2][:, 0:G * MR].rearrange("p (m r) -> p m r", r=GQ),
                                    eye8.unsqueeze(1).to_broadcast([P, G * M, GQ]), ALU.mult)\
                        .then_inc(s["scores_drained"], 1)
                    dve.wait_ge(s["scores_drained"], TB * t + b + 1)
                    V.tensor_reduce(sc[:, b * G:(b + 1) * G, :].rearrange("p g m -> p (g m)"),
                                    masked[:, b % 2, :, :], X, ALU.add).then_inc(s["sc_set"], 1)

            def softmax_off(t):
                dve.wait_ge(s["sc_set"], TB * t + TB)
                V.tensor_tensor(sc[:, :, :].rearrange("p (b g) m -> p b (g m)", b=TB),
                                sc[:, :, :].rearrange("p (b g) m -> p b (g m)", b=TB),
                                absent.unsqueeze(1).to_broadcast([P, TB, G * M]), ALU.add).then_inc(s["sc_added"], 1)
                dve.wait_ge(s["sc_added"], t + 1)
                V.tensor_reduce(sc_max[:, :], sc[:, :, :], X, ALU.max).then_inc(s["max_set"], 1)
                dve.wait_ge(s["max_set"], t + 1)
                V.tensor_tensor(sc_off[:, :, :], sc[:, :, :],
                                sc_max[:, :].unsqueeze(2).to_broadcast([P, TB * G, M]), ALU.subtract)\
                    .then_inc(s["off_set"], 1)

            def softmax_prob(t):
                dve.wait_ge(s["exp_set"], t + 1)
                V.tensor_reduce(sc_sum[:, :], expd[:, :, :], X, ALU.add).then_inc(s["sum_set"], 1)
                dve.wait_ge(s["sum_set"], t + 1)
                V.reciprocal(sc_inv[:, :], sc_sum[:, :]).then_inc(s["inv_set"], 1)
                dve.wait_ge(s["inv_set"], t + 1)
                V.tensor_tensor(prob[:, :, :], expd[:, :, :],
                                sc_inv[:, :].unsqueeze(2).to_broadcast([P, TB * G, M]), ALU.mult)\
                    .then_inc(s["prob_set"], 1)
                dve.wait_ge(s["prob_set"], t + 1)
                for j in range(2):
                    at = slice(8 * j, 8 * j + 8)
                    V.tensor_tensor(spread[:, at, :, :],
                                    prob[:, at, 0:M - 1].unsqueeze(3).to_broadcast([P, 8, M - 1, GQ]),
                                    eye8.unsqueeze(1).unsqueeze(1).to_broadcast([P, 8, M - 1, GQ]), ALU.mult)\
                        .then_inc(s["spread_set"], 1)

            def take_prob_t(t):
                dve.wait_ge(s["prob9_filled"], t + 1)
                V.tensor_tensor(prob9[:, :, :], ps_z[0:TB, 0:H].unsqueeze(1).to_broadcast([TB, TB, H]),
                                ident[0:TB, 0:TB].unsqueeze(2).to_broadcast([TB, TB, H]), ALU.mult)\
                    .then_inc(s["prob9_set"], 1)
                for j in range(2):
                    dve.wait_ge(s["prob_t_filled"], 2 * t + j + 1)
                    V.tensor_copy(prob_t[:, 4 * j:4 * j + 4, :], ps_s[j][:, :]).then_inc(s["prob_t_set"], 1)

            def back_x1(t, drained):
                dve.wait_ge(s["x_bo_set"], t + 1)
                dve.wait_ge(s["ring_drained"], drained)
                V.tensor_tensor(x1[:, :], x_bo[:, :], o_raw[:, :], ALU.add).then_inc(s["x1_set"], 1)
                dve.wait_ge(s["x1_set"], t + 1)
                moments(x1[:, :], b_stats, "b_stats_first" if isinstance(t, int) else "b_stats_set",
                        (1 if t == 0 else 2) if isinstance(t, int) else t, b_mv, "b_mv_set")

            def back_norm(u):
                normalise(u + 1, x1[:, :], b_mv, b_rstd, "b_rstd_set", b_xn[:, :], "b_xn_set")

            def back_bias(u):
                dve.wait_ge(s["qk_filled"], u + 1)
                V.tensor_tensor(qk[:, :], ps_x[:, :], sbias[:, 0:2 * D], ALU.add).then_inc(s["qk_set"], 1)
                dve.wait_ge(s["qk_set"], u + 1)
                V.tensor_tensor(r_b[:, :], qk[:, :], rope_b[:, :], ALU.mult).then_inc(s["r_b_set"], 1)
                dve.wait_ge(s["v_filled"], u + 1)
                V.tensor_tensor(v[:, :], ps_y[:, 0:D], sbias[:, 2 * D:3 * D], ALU.add).then_inc(s["v_set"], 1)

            def back_rope(u):
                dve.wait_ge(s["r_a_set"], u + 1)
                dve.wait_ge(s["r_b_set"], u + 1)
                rb = r_b[:, :].rearrange("p (n two) -> p n two", two=2)
                V.tensor_tensor(roped[:, :].rearrange("p (n two) -> p n two", two=2),
                                r_a[:, :].rearrange("p (n two) -> p n two", two=2),
                                rb[:, :, ::-1], ALU.add).then_inc(s["roped_set"], 1)
                dve.wait_ge(s["roped_set"], u + 1)
                dve.wait_ge(s["sq_rinv_set"], u + 1)
                for i in range(2):
                    V.tensor_scalar(feat[:, i * D:(i + 1) * D], roped[:, i * D:(i + 1) * D], sq_rinv[:, i:i + 1], 0.0,
                                    ALU.mult, ALU.max).then_inc(s["feat_set"], 1)

            def back_state(u):
                dve.wait_ge(s["kv_filled"], u + 1)
                for k in range(KD):
                    V.tensor_tensor(state[:, k, :, 0:P], (ps_x, ps_y)[k][:, :].rearrange("p (b e) -> p b e", b=TB),
                                    same_head.unsqueeze(1).to_broadcast([P, TB, P]), ALU.mult)\
                        .then_inc(s["state_set"], 1)
                dve.wait_ge(s["qf_t_set"], u + 1)
                for k in range(KD):
                    V.tensor_tensor(state[:, k, :, P:KVW],
                                    ps_z[:, D + k * TB:D + (k + 1) * TB].unsqueeze(2).to_broadcast([P, TB, HH]),
                                    of_head.unsqueeze(1).to_broadcast([P, TB, HH]), ALU.mult)\
                        .then_inc(s["state_set"], 1)

            def back_lin(u):
                dve.wait_ge(s["num_filled"], u + 1)
                num = ps_x[:, 0:KD * KVW].rearrange("p (k e) -> p k e", k=KD)
                V.tensor_scalar(den[:, :, :], num[:, :, P:KVW], LIN_EPS, None, ALU.add).then_inc(s["den_set"], 1)
                dve.wait_ge(s["den_set"], u + 1)
                V.reciprocal(den_inv[:, :, :], den[:, :, :]).then_inc(s["den_inv_set"], 1)
                dve.wait_ge(s["den_inv_set"], u + 1)
                for k in range(KD):
                    ins = V.tensor_tensor(lin[:, k * P:(k + 1) * P].rearrange("p (h e) -> p h e", e=SD),
                                          num[:, k, 0:P].rearrange("p (h e) -> p h e", e=SD),
                                          den_inv[:, k, :].unsqueeze(2).to_broadcast([P, HH, SD]), ALU.mult)
                ins.then_inc(s["lin_set"], 1)

            def back_y(u):
                dve.wait_ge(s["y_filled"], u + 1)
                V.tensor_tensor(y[:, :], ps_y[:, 0:D], sbo[:, :], ALU.add).then_inc(s["y_set"], 1)
                dve.wait_ge(s["y_set"], u + 1)
                V.tensor_tensor(y_g[:, :], y[:, :], gout[:, :], ALU.mult).then_inc(s["y_g_set"], 1)

            def back_x2(u):
                dve.wait_ge(s["y_rinv_set"], u + 1)
                dve.wait_ge(s["y_g_set"], u + 1)
                V.scalar_tensor_tensor(x2[:, :], y_g[:, :], y_rinv[:, 0:1], x1[:, :], ALU.mult, ALU.add)\
                    .then_inc(s["x2_set"], 1)
                dve.wait_ge(s["x2_set"], u + 1)
                moments(x2[:, :], f_stats, "f_stats_set", u + 1, f_mv, "f_mv_set")
                normalise(u + 1, x2[:, :], f_mv, f_rstd, "f_rstd_set", f_xn[:, :], "f_xn_set")

            def back_quant(u):
                dve.wait_ge(s["f_xn_set"], u + 1)
                V.tensor_reduce(amax[:, :], f_xn[:, :], X, ALU.max, apply_absolute_value=True).then_inc(s["amax_set"], 1)
                dve.wait_ge(s["amax_set"], u + 1)
                V.tensor_scalar(amax_g[:, :], amax[:, :], 1e-5, None, ALU.max).then_inc(s["amax_g_set"], 1)
                dve.wait_ge(s["amax_g_set"], u + 1)
                V.reciprocal(act_inv[:, :], amax_g[:, :]).then_inc(s["act_inv_set"], 1)
                dve.wait_ge(s["act_inv_set"], u + 1)
                V.tensor_scalar(act_scale[:, :], act_inv[:, :], 127.0, None, ALU.mult).then_inc(s["act_scale_set"], 1)
                dve.wait_ge(s["act_scale_set"], u + 1)
                V.tensor_scalar(f_q[:, :], f_xn[:, :], act_scale[:, 0:1], -128.0, ALU.mult, ALU.max)\
                    .then_inc(s["f_q_set"], 1)
                V.reciprocal(dq[:, :], act_scale[:, :]).then_inc(s["dq_set"], 1)
                dve.wait_ge(s["f_q_set"], u + 1)
                V.tensor_scalar(f_r[:, :], f_q[:, :], 127.0, ROUND, ALU.min, ALU.add).then_inc(s["f_r_set"], 1)
                dve.wait_ge(s["dq_set"], u + 1)
                V.tensor_tensor(dq_w[:, :], dq[:, :], wscale[:, :], ALU.mult).then_inc(s["dq_w_set"], 1)
                dve.wait_ge(s["f_r_set"], u + 1)
                V.tensor_scalar(f_i[:, :], f_r[:, :], -ROUND, None, ALU.add).then_inc(s["f_i_set"], 1)

            def back_x3(u):
                dve.wait_ge(s["f_filled"], u + 1)
                dve.wait_ge(s["dq_w_set"], u + 1)
                dve.wait_ge(s["x2_b_set"], u + 1)
                if not (isinstance(u, int) and u == 0):
                    dve.wait_ge(s["out_stored"], 16 * u)
                V.scalar_tensor_tensor(x3[:, :], ps_x[:, 0:D], dq_w[:, 0:1], x2_b[:, :], ALU.mult, ALU.add)\
                    .then_inc(s["x3_set"], 1)

            def step(t, front, back):
                u = t - 1
                n = STEP * (t + 1) + FRONT if front else STEP * (t + 1)
                if front:
                    front_moments(t + 1)
                take_scores(t, (0,))
                if front:
                    front_norm(t + 1)
                if back:
                    back_norm(u)
                take_scores(t, (1, 2, 3))
                softmax_off(t)
                softmax_prob(t)
                if back:
                    back_bias(u)
                take_prob_t(t)
                if back:
                    back_rope(u)
                    back_state(u)
                    back_lin(u)
                    back_y(u)
                    back_x2(u)
                    back_quant(u)
                back_x1(t, n)
                if back:
                    back_x3(u)

            dve.wait_ge(s["x0_in"], 16)
            front_moments(0)
            front_norm(0)
            dve.wait_ge(s["const_in"], 16)
            dve.wait_ge(s["x_in"], 16)
            step(0, True, False)
            V.tensor_copy(ident16[:, :], ident).then_inc(s["ident16_set"], 1)
            dve.wait_ge(s["ffn_in"], 48)
            for c in range(4):
                V.tensor_scalar(codes[:, :, c, :], packed[:, :, :], 2 * c, 3, ALU.logical_shift_right,
                                ALU.bitwise_and).then_inc(s["codes_set"], 1)
            dve.wait_ge(s["codes_set"], 4)
            V.tensor_scalar(fw[:, :, :].rearrange("p k n -> p (k n)"), codes[:, :, :, :].rearrange("p k c n -> p (k c n)"),
                            -1.0, None, ALU.add).then_inc(s["fw_set"], 1)
            dve.wait_ge(s["self_in"], 16 * 7)
            dve.wait_ge(s["rope_set"], 5)
            with dve.Fori(1, TILES - 1) as t:
                step(t, True, True)
            step(TILES - 1, False, True)
            u = TILES - 1
            for stage in (back_norm, back_bias, back_rope, back_state, back_lin, back_y, back_x2, back_quant, back_x3):
                stage(u)

        @block.gpsimd
        def _(pool):
            g = nc.gpsimd

            def rsqrt(t1, o, o_s, mean, mean_s, src, src_s, count, eps, n=1):
                pool.wait_ge(s[src_s], count * t1)
                g.tensor_tensor(mean, src, eps[:, 0:n], ALU.add).then_inc(s[mean_s], 1)
                pool.wait_ge(s[mean_s], t1)
                g.tensor_tensor(o, mean, minus_half[:, 0:n], ALU.pow).then_inc(s[o_s], 1)

            def norm_front(t):
                rsqrt(t + 1, ln_rstd[:, :], "ln_rstd_set", ln_var[:, :], "ln_var_set", ln_mv[:, 1:2], "ln_mv_set",
                      1, ln_eps)

            def add_mix9(t, drained):
                pool.wait_ge(s["mix9_set"], t + 1)
                pool.wait_ge(s["ring_drained"], drained)
                for k in range(KD):
                    at = mix[:, k, :, 0, :, 0]
                    ins = g.tensor_tensor(at, at, mix9[:, k, :, :], ALU.add)
                ins.then_inc(s["mix_set"], 1)

            def residual(t):
                if not (isinstance(t, int) and t == 0):
                    pool.wait_ge(s["x1_set"], t)
                g.tensor_tensor(x_bo[:, :], x_all[:, t, :], bo[:, :], ALU.add).then_inc(s["x_bo_set"], 1)

            def back_norm(u):
                rsqrt(u + 1, b_rstd[:, :], "b_rstd_set", b_var[:, :], "b_var_set", b_mv[:, 1:2], "b_mv_set",
                      1, ln_eps)

            def back_rope(u):
                pool.wait_ge(s["qk_set"], u + 1)
                g.tensor_tensor(r_a[:, :], qk[:, :], rope_a[:, :], ALU.mult).then_inc(s["r_a_set"], 1)
                rsqrt(u + 1, sq_rinv[:, :], "sq_rinv_set", sq_mean[:, :], "sq_mean_set", sq[:, :], "sq_set",
                      2, rms_eps, 2)
                pool.wait_ge(s["v_set"], u + 1)
                g.tensor_tensor(v_of[:, :, :], v[:, :].unsqueeze(1).to_broadcast([P, TB, D]),
                                of_batch.unsqueeze(2).to_broadcast([P, TB, D]), ALU.mult).then_inc(s["v_of_set"], 1)

            def back_y(u):
                rsqrt(u + 1, y_rinv[:, :], "y_rinv_set", y_mean[:, :], "y_mean_set", y_sq[:, :], "y_sq_set",
                      1, rms_eps)

            def back_f(u):
                rsqrt(u + 1, f_rstd[:, :], "f_rstd_set", f_var[:, :], "f_var_set", f_mv[:, 1:2], "f_mv_set",
                      1, ln_eps)
                pool.wait_ge(s["x2_set"], u + 1)
                g.tensor_tensor(x2_b[:, :], x2[:, :], fbias[:, :], ALU.add).then_inc(s["x2_b_set"], 1)

            def step(t, front, back):
                u = t - 1
                n = STEP * t + FRONT
                if back:
                    back_norm(u)
                if front:
                    norm_front(t + 1)
                    n = n + FRONT
                residual(t)
                if back:
                    back_rope(u)
                add_mix9(t, n + J_MIX // 2)
                if back:
                    back_y(u)
                    back_f(u)

            g.memset(minus_half[:, :], -0.5).then_inc(s["half_set"], 1)
            g.memset(ln_eps[:, :], LN_EPS).then_inc(s["half_set"], 1)
            g.memset(rms_eps[:, :], RMS_EPS * D).then_inc(s["half_set"], 1)
            pool.wait_ge(s["half_set"], 3)
            norm_front(0)
            pool.wait_ge(s["ln_rstd_set"], 1)
            g.memset(wk[64:128, 0:H:2, :], 0.0).then_inc(s["zeros_set"], 1)
            pool.wait_ge(s["zeros_set"], 1)
            g.memset(wk[0:64, 1:H:2, :], 0.0).then_inc(s["zeros_set"], 1)
            pool.wait_ge(s["zeros_set"], 2)
            g.memset(keys_t[:, :, :, NKV:KEYS], 0.0).then_inc(s["pads_set"], 1)
            pool.wait_ge(s["x0_in"], 16)
            pool.wait_ge(s["x_in"], 16)
            pool.wait_ge(s["bo_in"], 16)
            step(0, True, False)
            pool.wait_ge(s["self_in"], 16 * 7)
            pool.wait_ge(s["const_in"], 16)
            pool.wait_ge(s["ffn_in"], 48)
            for i in range(2):
                half = slice(i * D, (i + 1) * D)
                g.tensor_tensor(rope_a[:, half], gains[:, half], const[:, C_COS:C_COS + D], ALU.mult)\
                    .then_inc(s["rope_set"], 1)
                g.tensor_tensor(rope_b[:, half], gains[:, half], const[:, C_SIN:C_SIN + D], ALU.mult)\
                    .then_inc(s["rope_set"], 1)
            g.tensor_tensor(gout[:, :], gout[:, :], const[:, C_ROOT:C_ROOT + 1].to_broadcast([P, D]), ALU.mult)\
                .then_inc(s["rope_set"], 1)
            pool.wait_ge(s["rope_set"], 5)
            with pool.Fori(1, TILES - 1) as t:
                step(t, True, True)
            step(TILES - 1, False, True)
            for stage in (back_norm, back_rope, back_y, back_f):
                stage(TILES - 1)


def kernel(x, ctx_1024, L0_xattn_Wq, L0_xattn_Wkv, L0_xattn_Wout, L0_xattn_bout, L0_attn_Wqkv, L0_attn_bqkv,
           L0_attn_gq, L0_attn_gk, L0_attn_Wout, L0_attn_bout, L0_attn_gout, L0_ffn_packed_weight,
           L0_ffn_weight_scale, L0_ffn_bias):
    import concourse.bacc as _bacc
    from concourse.bass_utils import run_bass_kernel_spmd as _run

    c = np.asarray(ctx_1024).reshape(TILES, TB, NKV, D)
    wkv = np.asarray(L0_xattn_Wkv)
    by_group = c[:, :, :NKV - 1, :].reshape(TILES, TB, M - 1, 2, 2, GQ, D).transpose(0, 4, 2, 5, 1, 3, 6)
    arrays = {
        "x": np.asarray(x).reshape(BATCH * NQ, D),
        "ctx_t": c.reshape(TILES, TB, NKV, KD, P).transpose(0, 4, 3, 1, 2).reshape(TILES, P, KD * TB, NKV),
        "ctx_k": by_group.reshape(TILES, P, TB, 2, D),
        "ctx_9": c[:, :, NKV - 1, :],
        "const": constants(),
        "wq": L0_xattn_Wq, "wk_t": wkv[:, :INNER].T, "wv": wkv[:, INNER:], "wo": L0_xattn_Wout, "bo": L0_xattn_bout,
        "swqkv_t": np.asarray(L0_attn_Wqkv).T, "sbqkv": L0_attn_bqkv, "sgq": L0_attn_gq, "sgk": L0_attn_gk,
        "swo_t": np.asarray(L0_attn_Wout).T, "sbo": L0_attn_bout, "sgout": L0_attn_gout,
        "packed_t": np.asarray(L0_ffn_packed_weight).reshape(64, D).T,
        "wscale": L0_ffn_weight_scale, "fbias": L0_ffn_bias,
    }
    nc = _bacc.Bacc("TRN2", target_bir_lowering=False, num_devices=1)
    ins, given = {}, {}
    for name, v in arrays.items():
        v = np.ascontiguousarray(v)
        given[f"in_{name}"] = v
        ins[name] = nc.dram_tensor(f"in_{name}", v.shape, mybir.dt.from_np(v.dtype), kind="ExternalInput").ap()
    out = nc.dram_tensor("out", (TILES, P, D), F32, kind="ExternalOutput").ap()
    build(nc, ins, out)
    r = _run(nc, [given], core_ids=[0])
    return r.results[0]["out"].reshape(BATCH, NQ, D)
```

```python
from contextlib import ExitStack

import numpy as np

import concourse.bass as bass
from concourse import mybir

P = 128
D = 256
KD = D // P
BATCH, NQ, NKV = 32, 32, 257
TILES = BATCH * NQ // P
TB = P // NQ
H, DH = 16, 64
INNER = H * DH
HP = H // 2
GQ = 8
G = NQ // GQ
M = NKV // NQ + 1
MR = M * GQ
KEYS = M * NQ
SH, SD = 16, 16
HH = SH // KD
KVW = P + HH
SCALE = float(DH) ** -0.5
LN_EPS, RMS_EPS, LIN_EPS = 1e-5, 1.1920929e-07, 1e-6
NEG = -1e30
ROUND = float(3 << 22)

F32 = mybir.dt.float32
F32R = mybir.dt.float32r
BF16 = mybir.dt.bfloat16
I32 = mybir.dt.int32
ALU = mybir.AluOpType
ACT = mybir.ActivationFunctionType
X = mybir.AxisListType.X

RING = 3
J_Q, J_MIX, J_V = 2, 8, 2
STEP = J_Q + J_MIX + J_V
assert STEP % RING == 0
VRING = 2
J_S, J_QT = TB, 16
VSTEP = J_S + J_QT
assert VSTEP % VRING == 0 and J_QT % VRING == 0

C_ID = 0
C_BD = C_ID + P
C_EYE = C_BD + P
C_ABSENT = C_EYE + GQ
C_B = C_ABSENT + G
C_H = C_B + TB
C_ROOT = C_H + HH
C_W = C_ROOT + 1


def constants():
    c = np.zeros((P, C_W), np.float32)
    p = np.arange(P)
    c[:, C_ID:C_ID + P] = np.eye(P)
    c[:, C_BD:C_BD + P] = p[:, None] // SD == p[None, :] // SD
    c[:, C_ROOT] = float(D) ** 0.5
    c[:, C_EYE:C_EYE + GQ] = p[:, None] % GQ == np.arange(GQ)[None, :]
    c[:, C_ABSENT:C_ABSENT + G] = NEG
    c[p % GQ == 0, C_ABSENT] = 0.0
    c[:, C_B:C_B + TB] = p[:, None] // NQ == np.arange(TB)[None, :]
    c[:, C_H:C_H + HH] = p[:, None] // SD == np.arange(HH)[None, :]
    return c


def rope_table():
    freq = 1.0 / 10000.0 ** (np.arange(0, SD, 2) / SD)
    angle = np.repeat((np.arange(P) % NQ)[:, None] * freq[None, :], 2, axis=1)
    sign = np.where(np.arange(SD) % 2 == 0, 1.0, -1.0)
    root = float(D) ** 0.5
    return np.concatenate([np.tile(np.cos(angle) * root, (1, SH)), np.tile(np.sin(angle) * sign * root, (1, SH))],
                          axis=1).astype(np.float32)


def build(nc, a, out):
    with ExitStack() as ctx:
        def sb(name, shape, dt=F32):
            return ctx.enter_context(nc.sbuf_tensor(name, shape, dt))

        def ps(name):
            return ctx.enter_context(nc.psum_tensor(name, [P, 512], F32))

        def sem(name):
            return ctx.enter_context(nc.semaphore(name))

        const = sb("const", [P, C_W])
        ident = const[:, C_ID:C_ID + P]
        same_head = const[:, C_BD:C_BD + P]
        eye8 = const[:, C_EYE:C_EYE + GQ]
        absent = const[:, C_ABSENT:C_ABSENT + G]
        of_batch = const[:, C_B:C_B + TB]
        of_head = const[:, C_H:C_H + HH]
        ident16 = sb("ident16", [P, P], BF16)
        wq = sb("wq", [P, KD, INNER])
        wk_hl = sb("wk_hl", [P, H, D], F32R)
        wv = sb("wv", [P, KD, INNER])
        wo_hi, wo_lo = sb("wo_hi", [P, HP, D], F32R), sb("wo_lo", [P, HP, D], F32R)
        bo = sb("bo", [P, D])
        sw_hi, sw_lo = sb("sw_hi", [P, KD, 3 * D], F32R), sb("sw_lo", [P, KD, 3 * D], F32R)
        sbias = sb("sbias", [P, 3 * D])
        rope_a = sb("rope_a", [P, 2 * D])
        rope_b = sb("rope_b", [P, 2 * D])
        swo = sb("swo", [P, KD, D])
        sbo = sb("sbo", [P, D])
        gout = sb("gout", [P, D])
        fw = sb("fw", [P, KD, D], BF16)
        wscale = sb("wscale", [P, 1])
        fbias = sb("fbias", [P, D])
        minus_half = sb("minus_half", [P, 2])
        ln_eps = sb("ln_eps", [P, 2])
        rms_eps = sb("rms_eps", [P, 2])

        x_all = sb("x_all", [P, TILES, D])
        keys_t = sb("keys_t", [P, KD, TB, KEYS])
        keys = sb("keys", [P, TB, 2, D])
        key9 = sb("key9", [TB, D])
        ln_stats = sb("ln_stats", [P, TILES, 6])
        ln_mv = sb("ln_mv", [P, TILES, 2])
        ln_var = sb("ln_var", [P, TILES])
        ln_rstd = sb("ln_rstd", [P, TILES, 1])
        xn = sb("xn", [P, D])
        xn_t = sb("xn_t", [P, KD, P])
        q_hl = sb("q_hl", [P, H, 2, P], F32R)
        qt = sb("qt", [P, KD, TB * G, H, GQ])
        sc = sb("sc", [P, TB * G, M])
        sc_max = sb("sc_max", [P, TB * G])
        sc_off = sb("sc_off", [P, TB * G, M])
        expd = sb("expd", [P, TB * G, M])
        sc_sum = sb("sc_sum", [P, TB * G])
        sc_inv = sb("sc_inv", [P, TB * G])
        prob = sb("prob", [P, TB * G, M])
        spread = sb("spread", [P, TB * G, M - 1, GQ])
        prob9 = sb("prob9", [TB, TB, H])
        masked = sb("masked", [P, 2, G * M, GQ])
        prob_t = sb("prob_t", [P, 2 * TB, 2, P])
        mix9 = sb("mix9", [P, KD, TB, H])
        mix = sb("mix", [P, KD, TB, G, H, GQ])
        att_hi, att_lo = sb("att_hi", [P, HP, P], F32R), sb("att_lo", [P, HP, P], F32R)
        wk_raw, wo_raw = (mix[:, k, :, :, :, :].rearrange("p b g h q -> p (b g h q)")
                          .rearrange("p (c d) -> p c d", c=HP) for k in range(KD))
        x_bo = sb("x_bo", [P, D])

        x1 = sb("x1", [P, D])
        b_stats = sb("b_stats", [P, 6])
        b_mv = sb("b_mv", [P, 2])
        b_var = sb("b_var", [P, 1])
        b_rstd = sb("b_rstd", [P, 1])
        b_xn = sb("b_xn", [P, D])
        b_xn_hi, b_xn_lo = sb("b_xn_hi", [P, KD, P], F32R), sb("b_xn_lo", [P, KD, P], F32R)
        qk = sb("qk", [P, 2 * D])
        v = sb("v", [P, D])
        junk = sb("junk", [P, D])
        sq = sb("sq", [P, 2])
        sq_mean = sb("sq_mean", [P, 2])
        sq_rinv = sb("sq_rinv", [P, 2])
        feat = sb("feat", [P, 2 * D])
        r_b = sb("r_b", [P, 2 * D])
        v_of = sb("v_of", [P, TB, D])
        qf_t = sb("qf_t", [P, KD, P])
        state = sb("state", [P, KD, TB, KVW])
        den = sb("den", [P, KD, HH])
        den_inv = sb("den_inv", [P, KD, HH])
        gains, rope_tab = feat, r_b
        codes = qk[:, :].bitcast(I32).rearrange("p (k c n) -> p k c n", k=KD, c=4)
        packed = v[:, 0:KD * 64].bitcast(I32).rearrange("p (k n) -> p k n", k=KD)
        sw_raw = [v_of[:, 0:3, :].rearrange("p b n -> p (b n)"),
                  state[:, :, :, :].rearrange("p k b e -> p (k b e)")[:, 0:3 * D]]
        lin, lin_t = b_xn, qf_t
        y = sb("y", [P, D])
        y_sq = sb("y_sq", [P, 1])
        y_mean = sb("y_mean", [P, 1])
        y_rinv = sb("y_rinv", [P, 1])
        y_g = sb("y_g", [P, D])
        x2 = sb("x2", [P, D])
        x2_b = sb("x2_b", [P, D])
        f_stats = sb("f_stats", [P, 6])
        f_mv = sb("f_mv", [P, 2])
        f_var = sb("f_var", [P, 1])
        f_rstd = sb("f_rstd", [P, 1])
        f_xn = b_xn
        amax = sb("amax", [P, 1])
        amax_g = sb("amax_g", [P, 1])
        act_inv = sb("act_inv", [P, 1])
        act_scale = sb("act_scale", [P, 1])
        dq = sb("dq", [P, 1])
        dq_w = sb("dq_w", [P, 1])
        f_i = sb("f_i", [P, D], BF16)
        f_t = sb("f_t", [P, KD, P], BF16)
        x3 = sb("x3", [P, D])

        ring = [ps(f"ring{i}") for i in range(RING)]
        vring = [ps(f"vring{i}") for i in range(VRING)]
        ps_x, ps_y, ps_z = ps("ps_x"), ps("ps_y"), ps("ps_z")
        qt_banks = vring + [ps_x, ps_y, ps_z]

        names = """idle_set x0_in x_in ident_in const_in wq0_in wq1_in wk_in wv_in wo_in bo_in self_in ffn_in keys_t_in
            keys_in wk_hi_set wk_lo_set wk_lo_end_set pads_set half_set wo_hi_set wo_lo_set sw_in sw_hi_set
            sw_lo_set att_lo_set ident16_set rope_set codes_set fw_set ln_stats_set ln_mv_set ln_var_set
            ln_rstd_set xn_set xn_t_filled xn_t_set ring_filled ring_drained vring_filled vring_drained q_hi_set
            q_lo_set q_set prob_t_filled prob_t_set zeros_set qt_half_set o_filled sc_set sc_added max_set
            off_set exp_set sum_set inv_set prob_set spread_set prob9_filled prob9_set mix9_filled mix9_set
            mix_set x_bo_set x1_set b_stats_first b_stats_set b_mv_set b_var_set b_rstd_set b_xn_set
            b_xn_t_filled b_xn_hi_set b_xn_lo_set qk_filled v_filled qk_set v_set sq_set sq_mean_set sq_rinv_set
            r_a_set r_b_set roped_set feat_set v_of_set kv_filled qf_t_set state_set num_filled den_set
            den_inv_set lin_set lin_t_filled lin_t_set y_filled y_set y_sq_set y_mean_set y_rinv_set y_g_set
            x2_set x2_b_set f_stats_set f_mv_set f_var_set f_rstd_set f_xn_set amax_set amax_g_set act_inv_set
            act_scale_set dq_set dq_w_set f_q_set f_r_set f_i_set f_t_filled f_t_set f_filled x3_set
            out_stored""".split()
        s = {n: sem(n) for n in names}

        block = ctx.enter_context(nc.Block())

        @block.sync
        def _(sp):
            def load_keys_t(t):
                sp.dma_start(keys_t[:, :, :, 0:NKV].rearrange("p k b j -> p (k b) j"),
                             a["ctx_t"][t]).then_inc(s["keys_t_in"], 16)

            def load_keys(t):
                sp.dma_start(keys[:, :, :, :], a["ctx_k"][t]).then_inc(s["keys_in"], 16)
                sp.dma_start(key9[:, :], a["ctx_9"][t]).then_inc(s["keys_in"], 16)

            def broadcast(o, name, w, done):
                sp.dma_start(o, a[name].rearrange("(o n) -> o n", o=1).to_broadcast([P, w])).then_inc(s[done], 16)

            x_v = a["x"].rearrange("(t p) d -> p t d", p=P)
            wq_v = a["wq"].rearrange("(k p) n -> p k n", p=P)
            sp.dma_start(x_all[:, 0, :], x_v[:, 0, :]).then_inc(s["x0_in"], 16)
            sp.dma_start(const[:, 0:P], a["const"][:, 0:P]).then_inc(s["ident_in"], 16)
            sp.dma_start(wk_raw, a["wk_t"].rearrange("(c r) d -> r c d", r=P)).then_inc(s["wk_in"], 16)
            for j in range(J_Q):
                cols = slice(j * INNER // J_Q, (j + 1) * INNER // J_Q)
                sp.dma_start(wq[:, :, cols], wq_v[:, :, cols]).then_inc(s[f"wq{j}_in"], 16)
            sp.dma_start(const[:, P:C_W], a["const"][:, P:C_W]).then_inc(s["const_in"], 16)
            load_keys_t(0)
            sp.dma_start(wo_raw, a["wo"].rearrange("(c p) n -> p c n", p=P)).then_inc(s["wo_in"], 16)
            sp.dma_start(x_all[:, 1:TILES, :], x_v[:, 1:TILES, :]).then_inc(s["x_in"], 16)
            load_keys(0)
            broadcast(bo[:, :], "bo", D, "bo_in")
            sp.dma_start(wv[:, :, :], a["wv"].rearrange("(k p) n -> p k n", p=P)).then_inc(s["wv_in"], 16)
            broadcast(gains[:, 0:D], "sgq", D, "self_in")
            broadcast(gains[:, D:2 * D], "sgk", D, "self_in")
            broadcast(gout[:, :], "sgout", D, "self_in")
            sp.dma_start(rope_tab[:, :], a["rope"]).then_inc(s["self_in"], 16)
            for k in range(KD):
                sp.dma_start(sw_raw[k], a["swqkv_t"][k * P:(k + 1) * P, :]).then_inc(s["sw_in"], 16)
            sp.dma_start(swo[:, :, :], a["swo_t"].rearrange("(k p) n -> p k n", p=P)).then_inc(s["self_in"], 16)
            broadcast(sbias[:, :], "sbqkv", 3 * D, "self_in")
            broadcast(sbo[:, :], "sbo", D, "self_in")
            broadcast(fbias[:, :], "fbias", D, "ffn_in")
            broadcast(wscale[:, :], "wscale", 1, "ffn_in")
            sp.dma_start(packed, a["packed_t"].rearrange("(k p) n -> p k n", p=P)).then_inc(s["ffn_in"], 16)

            def stores(t):
                sp.wait_ge(s["x3_set"], t + 1)
                sp.dma_start(out[t], x3[:, :]).then_inc(s["out_stored"], 16)

            def step(t, back):
                sp.wait_ge(s["vring_filled"], VSTEP * t + (J_QT + J_S))
                load_keys_t(t + 1)
                sp.wait_ge(s["ring_filled"], STEP * t + (J_Q + J_Q + J_MIX))
                load_keys(t + 1)
                if back:
                    stores(t - 1)

            step(0, False)
            with sp.Fori(1, TILES - 1) as t:
                step(t, True)
            stores(TILES - 2)
            stores(TILES - 1)
            sp.wait_ge(s["out_stored"], 16 * TILES)

        @block.tensor
        def _(pe):
            mm = nc.tensor.matmul

            def product(o, left, right, start, stop):
                mm(o, left[0], right[0], start=start, stop=False)
                mm(o, left[0], right[1], start=False, stop=False)
                return mm(o, left[1], right[0], start=False, stop=stop)

            def ring_job(n, phase, c):
                if isinstance(n, int) and n + c < RING:
                    return ring[(phase + c) % RING]
                pe.wait_ge(s["ring_drained"], n + (c - RING + 1))
                return ring[(phase + c) % RING]

            def vring_job(vn, c, banks=vring):
                if not (isinstance(vn, int) and vn + c < len(banks)):
                    pe.wait_ge(s["vring_drained"], vn + (c - len(banks) + 1))
                return banks[c % len(banks)]

            def keep_clock(n, bank):
                for _ in range(n):
                    mm(bank[:, 0:KD * P], f_t[:, 0, :], f_t[:, :, :], start=True, stop=True)

            def transpose_xn(t):
                pe.wait_ge(s["xn_set"], t + 1)
                for k in range(KD):
                    last = nc.tensor.transpose(ps_z[:, k * P:(k + 1) * P], xn[:, k * P:(k + 1) * P], ident)
                last.then_inc(s["xn_t_filled"], 1)

            def q_job(t, n, phase, j, pairs=range(4)):
                if pairs[0] == 0:
                    pe.wait_ge(s["xn_t_set"], t + 1)
                    if isinstance(t, int) and t == 0:
                        pe.wait_ge(s[f"wq{j}_in"], 16)
                    ring_job(n, phase, j)
                bank = ring[(phase + j) % RING]
                for c in pairs:
                    hp = 4 * j + c
                    for k in range(KD):
                        last = mm(bank[:, c * P:(c + 1) * P], wq[:, k, hp * P:(hp + 1) * P], xn_t[:, k, :],
                                  start=(k == 0), stop=(k == KD - 1))
                if c == 3:
                    last.then_inc(s["ring_filled"], 1)

            def qt_jobs(t, vn, jobs, banks=vring):
                for j in jobs:
                    pair, k = j // KD, j % KD
                    bank = vring_job(vn, j, banks)
                    pe.wait_ge(s["q_hi_set"], J_Q * t + (pair // 4 + 1))
                    pe.wait_ge(s["q_set"], J_Q * t + (pair // 4 + 1))
                    for e in range(2):
                        h = 2 * pair + e
                        last = mm(bank[:, e * D:(e + 1) * D], wk_hl[:, h, k * P:(k + 1) * P], q_hl[:, h, :, :],
                                  start=True, stop=True)
                    last.then_inc(s["vring_filled"], 1)

            def scores(t, vn, batches):
                for b in batches:
                    if b == 0:
                        pe.wait_ge(s["keys_t_in"], 16 * t + 16)
                        pe.wait_ge(s["vring_drained"], vn)
                    bank = vring[b] if b < VRING else vring_job(vn, b)
                    for g in range(G):
                        for k in range(KD):
                            last = mm(bank[:, g * MR:(g + 1) * MR],
                                      qt[:, k, b * G + g, :, :].rearrange("p h q -> p (h q)"),
                                      keys_t[:, k, b, :].rearrange("p (m q) -> p m q", m=M)[:, :, g * GQ:(g + 1) * GQ],
                                      start=(k == 0), stop=(k == KD - 1))
                    last.then_inc(s["vring_filled"], 1)

            def prob9_job(t):
                if not (isinstance(t, int) and t == 0):
                    pe.wait_ge(s["b_xn_lo_set"], t)
                pe.wait_ge(s["prob_set"], 2 * t + 2)
                mm(ps_z[0:TB, 0:H], prob[:, 0:TB * G:G, M - 1], ident[:, 0:P:GQ], start=True, stop=True)\
                    .then_inc(s["prob9_filled"], 1)

            def transpose_prob(t, vn, j):
                pe.wait_ge(s["spread_set"], 2 * t + j + 1)
                bank = vring_job(vn, J_S + j)
                for c in range(4):
                    pair = 4 * j + c
                    last = nc.tensor.transpose(bank[:, c * P:(c + 1) * P],
                                               spread[:, 2 * pair:2 * pair + 2, :, :].rearrange("p g m r -> p (g m r)"),
                                               ident)
                last.then_inc(s["prob_t_filled"], 1)

            def mix9_job(t):
                pe.wait_ge(s["prob9_set"], t + 1)
                for k in range(KD):
                    last = mm(ps_z[:, k * TB * H:(k + 1) * TB * H], key9[:, k * P:(k + 1) * P],
                              prob9[:, :, :], start=True, stop=True)
                last.then_inc(s["mix9_filled"], 1)

            def mix_jobs(t, n, phase, front, jobs):
                for j in jobs:
                    b, k = j // KD, j % KD
                    bank = ring_job(n, phase, j)
                    if j == 0:
                        pe.wait_ge(s["keys_in"], 32 * t + 32)
                    if front and 0 <= j - (RING - J_Q) < J_Q:
                        pe.wait_ge(s["q_lo_set"], J_Q * t + (J_Q + 1 + j - (RING - J_Q)))
                    pe.wait_ge(s["prob_t_set"], 2 * t + 1 + b // 2)
                    for g2 in range(2):
                        last = mm(bank[:, g2 * D:(g2 + 1) * D], keys[:, b, g2, k * P:(k + 1) * P],
                                  prob_t[:, 2 * b + g2, :, :], start=True, stop=True)
                    last.then_inc(s["ring_filled"], 1)

            def value_start(t, n):
                pe.wait_ge(s["mix_set"], t + 1)
                pe.wait_ge(s["ring_drained"], n)
                if isinstance(t, int) and t == 0:
                    pe.wait_ge(s["wv_in"], 16)
                    pe.wait_ge(s["wo_lo_set"], 2)

            def value_job(n, phase, j, pairs):
                bank = ring[(phase + j) % RING]
                for c in pairs:
                    for k in range(KD):
                        for half in range(2):
                            h = 2 * (4 * j + c) + half
                            last = mm(bank[half * DH:(half + 1) * DH, c * P:(c + 1) * P],
                                      wv[:, k, h * DH:(h + 1) * DH],
                                      mix[:, k, :, :, h, :].rearrange("p b g q -> p (b g) q"),
                                      start=(k == 0), stop=(k == KD - 1), skip_group_check=True)
                if pairs[-1] == 3:
                    last.then_inc(s["ring_filled"], 1)

            def out_job(t, pairs):
                for c in pairs:
                    if c == 0 and not (isinstance(t, int) and t == 0):
                        pe.wait_ge(s["y_set"], t)
                    if c % 4 == 0:
                        pe.wait_ge(s["att_lo_set"], J_V * t + c // 4 + 1)
                    last = product(ps_y[:, 0:D], (att_hi[:, c, :], att_lo[:, c, :]), (wo_hi[:, c, :], wo_lo[:, c, :]),
                                   c == 0, c == HP - 1)
                if c == HP - 1:
                    last.then_inc(s["o_filled"], 1)

            def back_xn(u):
                pe.wait_ge(s["b_xn_set"], u + 1)
                for k in range(KD):
                    last = nc.tensor.transpose(ps_z[:, k * P:(k + 1) * P], b_xn[:, k * P:(k + 1) * P], ident)
                last.then_inc(s["b_xn_t_filled"], 1)

            def back_qk(u):
                pe.wait_ge(s["b_xn_lo_set"], u + 1)
                for k in range(KD):
                    last = product(ps_x[:, 0:2 * D], (b_xn_hi[:, k, :], b_xn_lo[:, k, :]),
                                   (sw_hi[:, k, 0:2 * D], sw_lo[:, k, 0:2 * D]), k == 0, k == KD - 1)
                last.then_inc(s["qk_filled"], 1)

            def back_v(u):
                for k in range(KD):
                    last = product(ps_y[:, 0:D], (b_xn_hi[:, k, :], b_xn_lo[:, k, :]),
                                   (sw_hi[:, k, 2 * D:3 * D], sw_lo[:, k, 2 * D:3 * D]), k == 0, k == KD - 1)
                last.then_inc(s["v_filled"], 1)

            def back_kv(u, more=True):
                pe.wait_ge(s["mix9_set"], u + 2 if more else u + 1)
                pe.wait_ge(s["feat_set"], 2 * u + 2)
                pe.wait_ge(s["v_of_set"], u + 1)
                for k in range(KD):
                    nc.tensor.transpose(ps_z[:, k * P:(k + 1) * P], feat[:, k * P:(k + 1) * P], ident)
                    kf = feat[:, D + k * P:D + (k + 1) * P]
                    mm(ps_z[:, D + k * TB:D + (k + 1) * TB], kf, of_batch, start=True, stop=True)
                    mm((ps_x, ps_y)[k][:, :], kf, v_of[:, :, k * P:(k + 1) * P], start=True, stop=True)\
                        .then_inc(s["kv_filled"], 1)

            def back_num(u):
                pe.wait_ge(s["qf_t_set"], u + 1)
                pe.wait_ge(s["state_set"], 4 * u + 4)
                for k in range(KD):
                    for b in range(TB):
                        last = mm(ps_x[b * NQ:(b + 1) * NQ, k * KVW:(k + 1) * KVW], qf_t[:, k, b * NQ:(b + 1) * NQ],
                                  state[:, k, b, :], start=True, stop=True)
                last.then_inc(s["num_filled"], 1)

            def back_lin(u):
                pe.wait_ge(s["lin_set"], u + 1)
                for k in range(KD):
                    last = nc.tensor.transpose(ps_z[:, k * P:(k + 1) * P], lin[:, k * P:(k + 1) * P], ident)
                last.then_inc(s["lin_t_filled"], 1)

            def back_out(u):
                pe.wait_ge(s["lin_t_set"], u + 1)
                for k in range(KD):
                    last = mm(ps_y[:, 0:D], lin_t[:, k, :], swo[:, k, :], start=(k == 0), stop=(k == KD - 1))
                last.then_inc(s["y_filled"], 1)

            def back_quant(u):
                pe.wait_ge(s["f_i_set"], u + 1)
                for k in range(KD):
                    last = nc.tensor.transpose(ps_z[:, k * 64:(k + 1) * 64].bitcast(BF16),
                                               f_i[:, k * P:(k + 1) * P], ident16[:, :])
                last.then_inc(s["f_t_filled"], 1)

            def back_ffn(u):
                pe.wait_ge(s["f_t_set"], u + 1)
                for k in range(KD):
                    last = mm(ps_x[:, 0:D], f_t[:, k, :], fw[:, k, :], start=(k == 0), stop=(k == KD - 1))
                last.then_inc(s["f_filled"], 1)

            def step(t, front, back):
                u = t - 1
                n, vn, phase = STEP * t + J_Q, VSTEP * t + J_QT, J_Q
                scores(t, vn, (0, 1))
                if front:
                    transpose_xn(t + 1)
                scores(t, vn, (2,))
                if back:
                    if front:
                        pe.wait_ge(s["xn_t_set"], t + 2)
                    back_xn(u)
                scores(t, vn, (3,))
                vq = vn + J_S

                def mix_(*jobs):
                    mix_jobs(t, n, phase, front, jobs)

                def qt_(*jobs):
                    if front:
                        qt_jobs(t + 1, vq, jobs)

                def back_(stage):
                    if back:
                        stage(u)

                if front:
                    q_job(t + 1, n, phase, 0)
                    transpose_prob(t, vn, 0)
                    back_(back_qk)
                    q_job(t + 1, n, phase, 1)
                    if not back:
                        pe.wait_ge(s["xn_t_set"], t + 2)
                    n, phase = n + J_Q, phase + J_Q
                    prob9_job(t)
                    transpose_prob(t, vn, 1)
                    back_(back_v)
                else:
                    back_qk(u)
                    transpose_prob(t, vn, 0)
                    back_v(u)
                    prob9_job(t)
                    transpose_prob(t, vn, 1)
                mix_(0, 1, 2)
                mix9_job(t)
                mix_(3, 4)
                back_(back_kv)
                qt_(0, 1)
                mix_(5)
                back_(back_num)
                qt_(2, 3)
                mix_(6)
                back_(back_lin)
                qt_(4, 5)
                mix_(7)
                back_(back_out)
                qt_(6, 7)
                value_start(t, n + J_MIX)
                value_job(n + J_MIX, phase + J_MIX, 0, (0, 1, 2, 3))
                qt_(8, 9)
                value_job(n + J_MIX, phase + J_MIX, 1, (0, 1))
                qt_(10, 11)
                value_job(n + J_MIX, phase + J_MIX, 1, (2, 3))
                qt_(12, 13)
                out_job(t, (0, 1, 2, 3, 4, 5))
                qt_(14, 15)
                back_(back_quant)
                out_job(t, (6, 7))
                back_(back_ffn)

            pe.wait_ge(s["idle_set"], 1)
            keep_clock(16, ps_x)
            pe.wait_ge(s["ident_in"], 16)
            transpose_xn(0)
            keep_clock(20, ps_x)
            for j in range(J_Q):
                q_job(0, 0, 0, j)
            keep_clock(8, ps_x)
            for half in range(2):
                pe.wait_ge(s["wk_lo_set"], 2 + half)
                if half:
                    pe.wait_ge(s["wk_lo_end_set"], 1)
                for j in range(half * J_QT // 2, (half + 1) * J_QT // 2):
                    qt_jobs(0, 0, (j,), qt_banks)
                    keep_clock(1, ring[2])
            keep_clock(8, ring[2])
            pe.wait_ge(s["pads_set"], 1)
            pe.wait_ge(s["zeros_set"], 1)
            pe.wait_ge(s["const_in"], 16)
            step(0, True, False)
            pe.wait_ge(s["self_in"], 16 * 7)
            pe.wait_ge(s["sw_lo_set"], KD)
            pe.wait_ge(s["ident16_set"], 1)
            pe.wait_ge(s["fw_set"], 1)
            with pe.Fori(1, TILES - 1) as t:
                step(t, True, True)
            step(TILES - 1, False, True)
            u = TILES - 1
            keep_clock(14, ring[0])
            back_xn(u)
            keep_clock(6, ring[0])
            back_qk(u)
            back_v(u)
            keep_clock(22, ring[0])
            back_kv(u, more=False)
            keep_clock(6, ring[0])
            back_num(u)
            keep_clock(8, ring[0])
            back_lin(u)
            keep_clock(4, ring[0])
            back_out(u)
            keep_clock(50, ring[0])
            back_quant(u)
            back_ffn(u)

        @block.scalar
        def _(act):
            def copy(o, i):
                return nc.scalar.activation(o, i, ACT.Copy)

            def drain(n, c, o, i):
                act.wait_ge(s["ring_filled"], n + (c + 1))
                copy(o, i).then_inc(s["ring_drained"], 1)

            def drain_xn(t):
                act.wait_ge(s["xn_t_filled"], t + 1)
                copy(xn_t[:, :, :], ps_z[:, 0:D]).then_inc(s["xn_t_set"], 1)

            def q_high(n, phase, j):
                act.wait_ge(s["ring_filled"], n + (j + 1))
                for e in range(2):
                    last = copy(q_hl[e * DH:(e + 1) * DH, 8 * j + e:8 * j + 8:2, 0, :],
                                ring[(phase + j) % RING][e * DH:(e + 1) * DH, :])
                last.then_inc(s["ring_drained"], 1)

            def q_high_twice(t, n, j):
                act.wait_ge(s["ring_drained"], n + (j + 1))
                for e in range(2):
                    last = copy(q_hl[(1 - e) * DH:(2 - e) * DH, 8 * j + e:8 * j + 8:2, 0, :],
                                q_hl[e * DH:(e + 1) * DH, 8 * j + e:8 * j + 8:2, 0, :].bitcast(F32))
                last.then_inc(s["q_hi_set"], 1)

            def drain_prob_t(t, j):
                act.wait_ge(s["prob_t_filled"], 2 * t + j + 1)
                for half in range(2):
                    rows = slice(half * 64, half * 64 + 64)
                    last = copy(prob_t[rows, 4 * j:4 * j + 4, half, :], vring[j][rows, :])
                last.then_inc(s["prob_t_set"], 1)

            def drain_qt(vn, jobs, banks=vring):
                for j in jobs:
                    pair, k = j // KD, j % KD
                    act.wait_ge(s["vring_filled"], vn + (j + 1))
                    copy(qt[:, k, :, 2 * pair:2 * pair + 2, :].rearrange("p g h q -> p h g q"),
                         banks[j % len(banks)][:, :].rearrange("p (h s g q) -> p h s g q", h=2, s=2, q=GQ)[:, :, 1])\
                        .then_inc(s["qt_half_set"], 1)

            def exponentials(t, j):
                act.wait_ge(s["off_set"], 2 * t + j + 1)
                at = slice(8 * j, 8 * j + 8)
                nc.scalar.activation(expd[:, at, :], sc_off[:, at, :], ACT.Exp, scale=SCALE).then_inc(s["exp_set"], 1)

            def drain_mix(n, phase, jobs):
                for j in jobs:
                    drain(n, j, mix[:, j % KD, j // KD, :, :, :].rearrange("p g h q -> p (g h q)"),
                          ring[(phase + j) % RING][:, :])

            def drain_values(n, phase, jobs):
                for j in jobs:
                    drain(n, j, att_hi[:, 4 * j:4 * j + 4, :], ring[(phase + j) % RING][:, :])

            def drain_mix9(t):
                act.wait_ge(s["mix9_filled"], t + 1)
                copy(mix9[:, :, :, :], ps_z[:, 0:KD * TB * H]).then_inc(s["mix9_set"], 1)

            def back_xn(u):
                act.wait_ge(s["b_xn_t_filled"], u + 1)
                copy(b_xn_hi[:, :, :], ps_z[:, 0:D]).then_inc(s["b_xn_hi_set"], 1)

            def back_squares(u):
                act.wait_ge(s["qk_set"], u + 1)
                for i in range(2):
                    if i:
                        act.wait_ge(s["sq_set"], 2 * u + 1)
                    elif not (isinstance(u, int) and u == 0):
                        act.wait_ge(s["y_sq_set"], u)
                    nc.scalar.activation(junk[:, :], qk[:, i * D:(i + 1) * D], ACT.Square,
                                         accum_out=sq[:, i:i + 1]).then_inc(s["sq_set"], 1)

            def back_values(u):
                act.wait_ge(s["v_set"], u + 1)
                for b in range(TB):
                    last = nc.scalar.activation(v_of[:, b, :], v[:, :], ACT.Copy, scale=of_batch[:, b:b + 1])
                last.then_inc(s["v_of_set"], 1)

            def back_qf(u):
                act.wait_ge(s["kv_filled"], KD * u + KD)
                copy(qf_t[:, :, :], ps_z[:, 0:D]).then_inc(s["qf_t_set"], 1)

            def back_lin(u):
                act.wait_ge(s["lin_t_filled"], u + 1)
                copy(lin_t[:, :, :], ps_z[:, 0:D]).then_inc(s["lin_t_set"], 1)

            def back_y(u):
                act.wait_ge(s["y_set"], u + 1)
                act.wait_ge(s["sq_set"], 2 * u + 2)
                nc.scalar.activation(junk[:, :], y[:, :], ACT.Square, accum_out=y_sq[:, :]).then_inc(s["y_sq_set"], 1)

            def back_quant(u):
                act.wait_ge(s["f_t_filled"], u + 1)
                copy(f_t[:, :, :], ps_z[:, 0:P].bitcast(BF16)).then_inc(s["f_t_set"], 1)

            def step(t, front, back):
                u = t - 1
                n, vq, phase = STEP * t + J_Q, VSTEP * t + (J_QT + J_S), J_Q
                if front:
                    drain_xn(t + 1)
                exponentials(t, 0)
                if back:
                    back_xn(u)
                else:
                    act.wait_ge(s["sw_in"], 16 * KD)
                    for k in range(KD):
                        copy(sw_hi[:, k, :], sw_raw[k]).then_inc(s["sw_hi_set"], 1)

                def mix_(*jobs):
                    drain_mix(n, phase, jobs)

                def qt_(*jobs):
                    if front:
                        drain_qt(vq, jobs)

                def back_(stage):
                    if back:
                        stage(u)

                nq = n
                exponentials(t, 1)
                if front:
                    q_high(n, phase, 0)
                drain_prob_t(t, 0)
                if front and back:
                    q_high_twice(t + 1, n, 0)
                    q_high(n, phase, 1)
                elif front:
                    q_high(n, phase, 1)
                    q_high_twice(t + 1, n, 0)
                if front:
                    n, phase = n + J_Q, phase + J_Q
                drain_prob_t(t, 1)
                back_(back_squares)
                if not back:
                    act.wait_ge(s["wo_lo_set"], 2)
                mix_(0, 1)
                if front:
                    q_high_twice(t + 1, nq, 1)
                mix_(2)
                drain_mix9(t)
                mix_(3, 4)
                back_(back_qf)
                qt_(0, 1)
                mix_(5)
                qt_(2, 3)
                mix_(6)
                back_(back_lin)
                qt_(4, 5)
                mix_(7)
                back_(back_y)
                qt_(6, 7)
                drain_values(n + J_MIX, phase + J_MIX, (0,))
                qt_(8, 9, 10, 11)
                drain_values(n + J_MIX, phase + J_MIX, (1,))
                qt_(12, 13, 14, 15)
                back_(back_quant)

            drain_xn(0)
            act.wait_ge(s["wk_in"], 16)
            for half in range(2):
                pairs = slice(4 * half, 4 * half + 4)
                for e in range(2):
                    rows = slice(e * DH, (e + 1) * DH)
                    copy(wk_hl[rows, 8 * half + e:8 * half + 8:2, :], wk_raw[rows, pairs, :])\
                        .then_inc(s["wk_hi_set"], 1)
            for j in range(J_Q):
                q_high(0, 0, j)
                q_high_twice(0, 0, j)
            drain_qt(0, range(J_QT), qt_banks)
            act.wait_ge(s["wo_in"], 16)
            copy(wo_hi[:, :, :], wo_raw).then_inc(s["wo_hi_set"], 1)
            step(0, True, False)
            with act.Fori(1, TILES - 1) as t:
                step(t, True, True)
            step(TILES - 1, False, True)
            u = TILES - 1
            for stage in (back_xn, back_squares, back_values, back_qf, back_lin, back_y, back_quant):
                stage(u)

        @block.vector
        def _(dve):
            V = nc.vector

            def moments(src, stats, stats_s, count, mv, mv_s):
                V.bn_stats(stats[:, :], src).then_inc(s[stats_s], 1)
                dve.wait_ge(s[stats_s], 1)
                dve.wait_ge(s[stats_s], count)
                V.bn_aggr(mv[:, :], stats[:, :]).then_inc(s[mv_s], 1)

            def normalise(t1, src, mv, rstd, rstd_s, o, o_s):
                dve.wait_ge(s[rstd_s], t1)
                V.tensor_scalar(o, src, mv[:, 0:1], rstd[:, 0:1], ALU.subtract, ALU.mult).then_inc(s[o_s], 1)

            def front_moments(tiles):
                for t in tiles:
                    V.bn_stats(ln_stats[:, t, :], x_all[:, t, :]).then_inc(s["ln_stats_set"], 1)
                for t in tiles:
                    dve.wait_ge(s["ln_stats_set"], t + 1)
                    V.bn_aggr(ln_mv[:, t, :], ln_stats[:, t, :]).then_inc(s["ln_mv_set"], 1)

            def front_norm(t):
                if not (isinstance(t, int) and t == 0):
                    dve.wait_ge(s["xn_t_filled"], t)
                if isinstance(t, int):
                    dve.wait_ge(s["ln_rstd_set"], t + 1)
                V.tensor_scalar(xn[:, :], x_all[:, t, :], ln_mv[:, t, 0:1], ln_rstd[:, t, :],
                                ALU.subtract, ALU.mult).then_inc(s["xn_set"], 1)

            def take_scores(t, vn, batches):
                for b in batches:
                    dve.wait_ge(s["vring_filled"], vn + (b + 1))
                    V.tensor_tensor(masked[:, b % 2, :, :],
                                    vring[b % VRING][:, 0:G * MR].rearrange("p (m r) -> p m r", r=GQ),
                                    eye8.unsqueeze(1).to_broadcast([P, G * M, GQ]), ALU.mult)\
                        .then_inc(s["vring_drained"], 1)
                    dve.wait_ge(s["vring_drained"], vn + (b + 1))
                    V.tensor_reduce(sc[:, b * G:(b + 1) * G, :].rearrange("p g m -> p (g m)"),
                                    masked[:, b % 2, :, :], X, ALU.add).then_inc(s["sc_set"], 1)

            def softmax_off(t, j):
                at = slice(8 * j, 8 * j + 8)
                dve.wait_ge(s["sc_set"], TB * t + 2 * j + 2)
                last_slot = sc[:, at, M - 1].rearrange("p (b g) -> p b g", b=2)
                V.tensor_tensor(last_slot, last_slot, absent.unsqueeze(1).to_broadcast([P, 2, G]), ALU.add)\
                    .then_inc(s["sc_added"], 1)
                dve.wait_ge(s["sc_added"], 2 * t + j + 1)
                V.tensor_reduce(sc_max[:, at], sc[:, at, :], X, ALU.max).then_inc(s["max_set"], 1)
                dve.wait_ge(s["max_set"], 2 * t + j + 1)
                V.tensor_tensor(sc_off[:, at, :], sc[:, at, :],
                                sc_max[:, at].unsqueeze(2).to_broadcast([P, 8, M]), ALU.subtract)\
                    .then_inc(s["off_set"], 1)

            def softmax_prob(t, j):
                at = slice(8 * j, 8 * j + 8)
                dve.wait_ge(s["exp_set"], 2 * t + j + 1)
                V.tensor_reduce(sc_sum[:, at], expd[:, at, :], X, ALU.add).then_inc(s["sum_set"], 1)
                dve.wait_ge(s["sum_set"], 2 * t + j + 1)
                V.reciprocal(sc_inv[:, at], sc_sum[:, at]).then_inc(s["inv_set"], 1)
                dve.wait_ge(s["inv_set"], 2 * t + j + 1)
                V.tensor_tensor(prob[:, at, :], expd[:, at, :],
                                sc_inv[:, at].unsqueeze(2).to_broadcast([P, 8, M]), ALU.mult)\
                    .then_inc(s["prob_set"], 1)
                dve.wait_ge(s["prob_set"], 2 * t + j + 1)
                V.tensor_tensor(spread[:, at, :, :],
                                prob[:, at, 0:M - 1].unsqueeze(3).to_broadcast([P, 8, M - 1, GQ]),
                                eye8.unsqueeze(1).unsqueeze(1).to_broadcast([P, 8, M - 1, GQ]), ALU.mult)\
                    .then_inc(s["spread_set"], 1)

            def take_prob9(t):
                dve.wait_ge(s["prob9_filled"], t + 1)
                V.tensor_tensor(prob9[:, :, :], ps_z[0:TB, 0:H].unsqueeze(1).to_broadcast([TB, TB, H]),
                                ident[0:TB, 0:TB].unsqueeze(2).to_broadcast([TB, TB, H]), ALU.mult)\
                    .then_inc(s["prob9_set"], 1)

            def back_x1(t):
                dve.wait_ge(s["x_bo_set"], t + 1)
                dve.wait_ge(s["o_filled"], t + 1)
                V.tensor_tensor(x1[:, :], ps_y[:, 0:D], x_bo[:, :], ALU.add).then_inc(s["x1_set"], 1)
                dve.wait_ge(s["x1_set"], t + 1)
                moments(x1[:, :], b_stats, "b_stats_first" if isinstance(t, int) else "b_stats_set",
                        (1 if t == 0 else 2) if isinstance(t, int) else t, b_mv, "b_mv_set")

            def back_norm(u):
                normalise(u + 1, x1[:, :], b_mv, b_rstd, "b_rstd_set", b_xn[:, :], "b_xn_set")

            def back_bias_qk(u):
                dve.wait_ge(s["qk_filled"], u + 1)
                V.tensor_tensor(qk[:, :], ps_x[:, :], sbias[:, 0:2 * D], ALU.add).then_inc(s["qk_set"], 1)

            def back_bias_v(u):
                dve.wait_ge(s["v_filled"], u + 1)
                V.tensor_tensor(v[:, :], ps_y[:, 0:D], sbias[:, 2 * D:3 * D], ALU.add).then_inc(s["v_set"], 1)

            def back_rope(u):
                dve.wait_ge(s["qk_set"], u + 1)
                V.tensor_tensor(r_b[:, :], qk[:, :], rope_b[:, :], ALU.mult).then_inc(s["r_b_set"], 1)
                dve.wait_ge(s["r_a_set"], u + 1)
                dve.wait_ge(s["r_b_set"], u + 1)
                rb = r_b[:, :].rearrange("p (n two) -> p n two", two=2)
                V.tensor_tensor(feat[:, :].rearrange("p (n two) -> p n two", two=2),
                                feat[:, :].rearrange("p (n two) -> p n two", two=2),
                                rb[:, :, ::-1], ALU.add).then_inc(s["roped_set"], 1)
                dve.wait_ge(s["roped_set"], u + 1)
                dve.wait_ge(s["sq_rinv_set"], u + 1)
                for i in range(2):
                    V.tensor_scalar(feat[:, i * D:(i + 1) * D], feat[:, i * D:(i + 1) * D], sq_rinv[:, i:i + 1], 0.0,
                                    ALU.mult, ALU.max).then_inc(s["feat_set"], 1)

            def back_state(u):
                for k in range(KD):
                    dve.wait_ge(s["kv_filled"], KD * u + k + 1)
                    V.tensor_tensor(state[:, k, :, 0:P], (ps_x, ps_y)[k][:, :].rearrange("p (b e) -> p b e", b=TB),
                                    same_head.unsqueeze(1).to_broadcast([P, TB, P]), ALU.mult)\
                        .then_inc(s["state_set"], 1)
                dve.wait_ge(s["qf_t_set"], u + 1)
                for k in range(KD):
                    V.tensor_tensor(state[:, k, :, P:KVW],
                                    ps_z[:, D + k * TB:D + (k + 1) * TB].unsqueeze(2).to_broadcast([P, TB, HH]),
                                    of_head.unsqueeze(1).to_broadcast([P, TB, HH]), ALU.mult)\
                        .then_inc(s["state_set"], 1)

            def back_lin(u):
                dve.wait_ge(s["num_filled"], u + 1)
                num = ps_x[:, 0:KD * KVW].rearrange("p (k e) -> p k e", k=KD)
                V.tensor_scalar(den[:, :, :], num[:, :, P:KVW], LIN_EPS, None, ALU.add).then_inc(s["den_set"], 1)
                dve.wait_ge(s["den_set"], u + 1)
                V.reciprocal(den_inv[:, :, :], den[:, :, :]).then_inc(s["den_inv_set"], 1)
                dve.wait_ge(s["den_inv_set"], u + 1)
                for k in range(KD):
                    ins = V.tensor_tensor(lin[:, k * P:(k + 1) * P].rearrange("p (h e) -> p h e", e=SD),
                                          num[:, k, 0:P].rearrange("p (h e) -> p h e", e=SD),
                                          den_inv[:, k, :].unsqueeze(2).to_broadcast([P, HH, SD]), ALU.mult)
                ins.then_inc(s["lin_set"], 1)

            def back_y(u):
                dve.wait_ge(s["y_filled"], u + 1)
                V.tensor_tensor(y[:, :], ps_y[:, 0:D], sbo[:, :], ALU.add).then_inc(s["y_set"], 1)
                dve.wait_ge(s["y_set"], u + 1)
                V.tensor_tensor(y_g[:, :], y[:, :], gout[:, :], ALU.mult).then_inc(s["y_g_set"], 1)

            def back_x2(u):
                dve.wait_ge(s["y_rinv_set"], u + 1)
                dve.wait_ge(s["y_g_set"], u + 1)
                V.scalar_tensor_tensor(x2[:, :], y_g[:, :], y_rinv[:, 0:1], x1[:, :], ALU.mult, ALU.add)\
                    .then_inc(s["x2_set"], 1)
                dve.wait_ge(s["x2_set"], u + 1)
                moments(x2[:, :], f_stats, "f_stats_set", u + 1, f_mv, "f_mv_set")

            def back_f_norm(u):
                normalise(u + 1, x2[:, :], f_mv, f_rstd, "f_rstd_set", f_xn[:, :], "f_xn_set")

            def back_scale(u):
                dve.wait_ge(s["f_xn_set"], u + 1)
                V.tensor_reduce(amax[:, :], f_xn[:, :], X, ALU.max, apply_absolute_value=True)\
                    .then_inc(s["amax_set"], 1)
                dve.wait_ge(s["amax_set"], u + 1)
                V.tensor_scalar(amax_g[:, :], amax[:, :], 1e-5, None, ALU.max).then_inc(s["amax_g_set"], 1)
                dve.wait_ge(s["amax_g_set"], u + 1)
                V.reciprocal(act_inv[:, :], amax_g[:, :]).then_inc(s["act_inv_set"], 1)
                dve.wait_ge(s["act_inv_set"], u + 1)
                V.tensor_scalar(act_scale[:, :], act_inv[:, :], 127.0, None, ALU.mult).then_inc(s["act_scale_set"], 1)

            def back_quant(u):
                dve.wait_ge(s["act_scale_set"], u + 1)
                V.tensor_scalar(f_xn[:, :], f_xn[:, :], act_scale[:, 0:1], -128.0, ALU.mult, ALU.max)\
                    .then_inc(s["f_q_set"], 1)
                V.reciprocal(dq[:, :], act_scale[:, :]).then_inc(s["dq_set"], 1)
                dve.wait_ge(s["f_q_set"], u + 1)
                V.tensor_scalar(f_xn[:, :], f_xn[:, :], 127.0, ROUND, ALU.min, ALU.add).then_inc(s["f_r_set"], 1)
                dve.wait_ge(s["dq_set"], u + 1)
                V.tensor_tensor(dq_w[:, :], dq[:, :], wscale[:, :], ALU.mult).then_inc(s["dq_w_set"], 1)
                dve.wait_ge(s["f_r_set"], u + 1)
                V.tensor_scalar(f_i[:, :], f_xn[:, :], -ROUND, None, ALU.add).then_inc(s["f_i_set"], 1)

            def back_x3(u):
                dve.wait_ge(s["f_filled"], u + 1)
                dve.wait_ge(s["dq_w_set"], u + 1)
                dve.wait_ge(s["x2_b_set"], u + 1)
                if not (isinstance(u, int) and u == 0):
                    dve.wait_ge(s["out_stored"], 16 * u)
                V.scalar_tensor_tensor(x3[:, :], ps_x[:, 0:D], dq_w[:, 0:1], x2_b[:, :], ALU.mult, ALU.add)\
                    .then_inc(s["x3_set"], 1)

            def q_low(n, phase, j):
                dve.wait_ge(s["ring_drained"], n + (j + 1))
                for e in range(2):
                    rows = slice(e * DH, (e + 1) * DH)
                    heads = slice(8 * j + e, 8 * j + 8, 2)
                    last = V.tensor_tensor(q_hl[rows, heads, 1, :],
                                           ring[(phase + j) % RING][rows, :].rearrange("p (c n) -> p c n", c=4),
                                           q_hl[rows, heads, 0, :].bitcast(F32), ALU.subtract)
                last.then_inc(s["q_lo_set"], 1)

            def q_low_twice(t, j):
                dve.wait_ge(s["q_lo_set"], J_Q * t + (j + 1))
                for e in range(2):
                    heads = slice(8 * j + e, 8 * j + 8, 2)
                    last = V.tensor_copy(q_hl[(1 - e) * DH:(2 - e) * DH, heads, 1, :],
                                         q_hl[e * DH:(e + 1) * DH, heads, 1, :].bitcast(F32))
                last.then_inc(s["q_set"], 1)

            def att_low(t, n, phase, j):
                dve.wait_ge(s["ring_drained"], n + (j + 1))
                V.tensor_tensor(att_lo[:, 4 * j:4 * j + 4, :], ring[(phase + j) % RING][:, :]
                                .rearrange("p (c n) -> p c n", c=4), att_hi[:, 4 * j:4 * j + 4, :].bitcast(F32),
                                ALU.subtract).then_inc(s["att_lo_set"], 1)

            def b_xn_low(u):
                dve.wait_ge(s["b_xn_hi_set"], u + 1)
                V.tensor_tensor(b_xn_lo[:, :, :].rearrange("p k n -> p (k n)"), ps_z[:, 0:D],
                                b_xn_hi[:, :, :].rearrange("p k n -> p (k n)").bitcast(F32), ALU.subtract)\
                    .then_inc(s["b_xn_lo_set"], 1)

            def wout_low(pairs):
                dve.wait_ge(s["wo_hi_set"], 1)
                V.tensor_tensor(wo_lo[:, pairs, :], wo_raw[:, pairs, :], wo_hi[:, pairs, :].bitcast(F32), ALU.subtract)\
                    .then_inc(s["wo_lo_set"], 1)

            def wqkv_low():
                dve.wait_ge(s["sw_hi_set"], KD)
                for k in range(KD):
                    V.tensor_tensor(sw_lo[:, k, :], sw_raw[k], sw_hi[:, k, :].bitcast(F32), ALU.subtract)\
                        .then_inc(s["sw_lo_set"], 1)

            def add_qt(t, jobs, banks=vring):
                for j in jobs:
                    pair, k = j // KD, j % KD
                    dve.wait_ge(s["qt_half_set"], J_QT * t + (j + 1))
                    at = qt[:, k, :, 2 * pair:2 * pair + 2, :].rearrange("p g h q -> p h g q")
                    V.tensor_tensor(at, banks[j % len(banks)][:, :]
                                    .rearrange("p (h s g q) -> p h s g q", h=2, s=2, q=GQ)[:, :, 0], at, ALU.add)\
                        .then_inc(s["vring_drained"], 1)

            def prepare_ffn():
                V.tensor_copy(ident16[:, :], ident).then_inc(s["ident16_set"], 1)
                dve.wait_ge(s["ffn_in"], 48)
                for c in range(4):
                    V.tensor_scalar(codes[:, :, c, :], packed, 2 * c, 3, ALU.logical_shift_right,
                                    ALU.bitwise_and).then_inc(s["codes_set"], 1)
                dve.wait_ge(s["codes_set"], 4)
                V.tensor_scalar(fw[:, :, :].rearrange("p k n -> p (k n)"),
                                codes.rearrange("p k c n -> p (k c n)"),
                                -1.0, None, ALU.add).then_inc(s["fw_set"], 1)

            def step(t, front, back):
                u = t - 1
                n, vn, phase = STEP * t + J_Q, VSTEP * t + J_QT, J_Q
                if front:
                    front_norm(t + 1)
                if not back:
                    wout_low(slice(0, 4))
                take_scores(t, vn, (0,))
                if back:
                    back_norm(u)
                take_scores(t, vn, (1,))
                if not back:
                    wout_low(slice(4, 8))
                softmax_off(t, 0)
                take_scores(t, vn, (2,))
                if back:
                    b_xn_low(u)
                softmax_prob(t, 0)
                take_scores(t, vn, (3,))
                if front:
                    n_v, phase_v = n + (J_Q + J_MIX), phase + J_Q + J_MIX
                else:
                    n_v, phase_v = n + J_MIX, phase + J_MIX

                def qt_(*jobs):
                    if front:
                        add_qt(t + 1, jobs)

                def back_(stage):
                    if back:
                        stage(u)

                softmax_off(t, 1)
                softmax_prob(t, 1)
                back_(back_bias_qk)
                if front:
                    q_low(n, phase, 0)
                take_prob9(t)
                back_(back_bias_v)
                if front:
                    q_low(n, phase, 1)
                back_(back_rope)
                if front:
                    q_low_twice(t + 1, 0)
                    q_low_twice(t + 1, 1)
                back_(back_state)
                if not back:
                    front_moments(range(2, TILES))
                qt_(0, 1)
                back_(back_lin)
                qt_(2, 3, 4, 5)
                if not back:
                    wqkv_low()
                back_(back_y)
                qt_(6, 7)
                back_(back_x2)
                qt_(8, 9)
                if not back:
                    prepare_ffn()
                back_(back_f_norm)
                att_low(t, n_v, phase_v, 0)
                qt_(10, 11)
                back_(back_scale)
                att_low(t, n_v, phase_v, 1)
                qt_(12, 13)
                back_(back_quant)
                qt_(14, 15)
                back_x1(t)
                back_(back_x3)

            V.memset(f_t[:, :, :], 0.0).then_inc(s["idle_set"], 1)
            dve.wait_ge(s["x0_in"], 16)
            front_moments((0,))
            front_norm(0)
            for half, e in ((0, 0), (0, 1), (1, 0)):
                pairs = slice(4 * half, 4 * half + 4)
                rows = slice(e * DH, (e + 1) * DH)
                heads = slice(8 * half + e, 8 * half + 8, 2)
                dve.wait_ge(s["wk_hi_set"], 2 * half + e + 1)
                V.tensor_tensor(wk_hl[(1 - e) * DH:(2 - e) * DH, heads, :], wk_raw[rows, pairs, :],
                                wk_hl[rows, heads, :].bitcast(F32), ALU.subtract).then_inc(s["wk_lo_set"], 1)
            for j in range(J_Q):
                q_low(0, 0, j)
                q_low_twice(0, j)
            add_qt(0, range(J_QT // 2), qt_banks)
            dve.wait_ge(s["x_in"], 16)
            front_moments((1,))
            add_qt(0, range(J_QT // 2, J_QT), qt_banks)
            dve.wait_ge(s["const_in"], 16)
            step(0, True, False)
            dve.wait_ge(s["ln_rstd_set"], 3)
            dve.wait_ge(s["self_in"], 16 * 7)
            dve.wait_ge(s["rope_set"], 5)
            with dve.Fori(1, TILES - 1) as t:
                step(t, True, True)
            step(TILES - 1, False, True)
            u = TILES - 1
            for stage in (back_norm, b_xn_low, back_bias_qk, back_bias_v, back_rope, back_state, back_lin, back_y,
                          back_x2, back_f_norm, back_scale, back_quant, back_x3):
                stage(u)

        @block.gpsimd
        def _(pool):
            g = nc.gpsimd

            def rsqrt(t1, o, o_s, mean, mean_s, src, src_s, count, eps, n=1):
                pool.wait_ge(s[src_s], count * t1)
                g.tensor_tensor(mean, src, eps[:, 0:n], ALU.add).then_inc(s[mean_s], 1)
                pool.wait_ge(s[mean_s], t1)
                g.tensor_tensor(o, mean, minus_half[:, 0:n], ALU.pow).then_inc(s[o_s], 1)

            def norm_front(t0, t1):
                part = slice(t0, t1)
                pool.wait_ge(s["ln_mv_set"], t1)
                g.tensor_tensor(ln_var[:, part], ln_mv[:, part, 1], ln_eps[:, 0:1].to_broadcast([P, t1 - t0]), ALU.add)\
                    .then_inc(s["ln_var_set"], 1)
                pool.wait_ge(s["ln_var_set"], min(t0, 2) + 1)
                g.tensor_tensor(ln_rstd[:, part, 0], ln_var[:, part],
                                minus_half[:, 0:1].to_broadcast([P, t1 - t0]), ALU.pow)\
                    .then_inc(s["ln_rstd_set"], 1)

            def add_mix9(t, drained):
                pool.wait_ge(s["mix9_set"], t + 1)
                for k in range(KD):
                    pool.wait_ge(s["ring_drained"], drained + (k - 1))
                    at = mix[:, k, :, 0, :, 0]
                    last = g.tensor_tensor(at, at, mix9[:, k, :, :], ALU.add)
                last.then_inc(s["mix_set"], 1)

            def residual(t):
                if not (isinstance(t, int) and t == 0):
                    pool.wait_ge(s["x1_set"], t)
                g.tensor_tensor(x_bo[:, :], x_all[:, t, :], bo[:, :], ALU.add).then_inc(s["x_bo_set"], 1)

            def back_norm(u):
                rsqrt(u + 1, b_rstd[:, :], "b_rstd_set", b_var[:, :], "b_var_set", b_mv[:, 1:2], "b_mv_set",
                      1, ln_eps)

            def back_rope(u, values=True):
                pool.wait_ge(s["qk_set"], u + 1)
                g.tensor_tensor(feat[:, :], qk[:, :], rope_a[:, :], ALU.mult).then_inc(s["r_a_set"], 1)
                if values:
                    pool.wait_ge(s["v_set"], u + 1)
                    g.tensor_tensor(v_of[:, :, :], v[:, :].unsqueeze(1).to_broadcast([P, TB, D]),
                                    of_batch.unsqueeze(2).to_broadcast([P, TB, D]), ALU.mult).then_inc(s["v_of_set"], 1)
                rsqrt(u + 1, sq_rinv[:, :], "sq_rinv_set", sq_mean[:, :], "sq_mean_set", sq[:, :], "sq_set",
                      2, rms_eps, 2)

            def back_y(u):
                rsqrt(u + 1, y_rinv[:, :], "y_rinv_set", y_mean[:, :], "y_mean_set", y_sq[:, :], "y_sq_set",
                      1, rms_eps)

            def back_f(u):
                rsqrt(u + 1, f_rstd[:, :], "f_rstd_set", f_var[:, :], "f_var_set", f_mv[:, 1:2], "f_mv_set",
                      1, ln_eps)
                pool.wait_ge(s["x2_set"], u + 1)
                g.tensor_tensor(x2_b[:, :], x2[:, :], fbias[:, :], ALU.add).then_inc(s["x2_b_set"], 1)

            def prepare_self():
                pool.wait_ge(s["self_in"], 16 * 7)
                pool.wait_ge(s["const_in"], 16)
                pool.wait_ge(s["ffn_in"], 48)
                for i in range(2):
                    half = slice(i * D, (i + 1) * D)
                    g.tensor_tensor(rope_a[:, half], gains[:, half], rope_tab[:, 0:D], ALU.mult)\
                        .then_inc(s["rope_set"], 1)
                    g.tensor_tensor(rope_b[:, half], gains[:, half], rope_tab[:, D:2 * D], ALU.mult)\
                        .then_inc(s["rope_set"], 1)
                g.tensor_tensor(gout[:, :], gout[:, :], const[:, C_ROOT:C_ROOT + 1].to_broadcast([P, D]), ALU.mult)\
                    .then_inc(s["rope_set"], 1)
                pool.wait_ge(s["rope_set"], 5)

            def step(t, front, back):
                u = t - 1
                n = STEP * t + J_Q
                if back:
                    back_norm(u)
                if front:
                    n = n + J_Q
                residual(t)
                if back:
                    back_rope(u)
                else:
                    prepare_self()
                    norm_front(2, TILES)
                add_mix9(t, n + J_MIX)
                if back:
                    back_y(u)
                    back_f(u)

            g.memset(minus_half[:, :], -0.5).then_inc(s["half_set"], 1)
            g.memset(ln_eps[:, :], LN_EPS).then_inc(s["half_set"], 1)
            g.memset(rms_eps[:, :], RMS_EPS * D).then_inc(s["half_set"], 1)
            pool.wait_ge(s["half_set"], 3)
            norm_front(0, 1)
            pool.wait_ge(s["ln_rstd_set"], 1)
            g.memset(prob_t[:, :, :, :], 0.0).then_inc(s["zeros_set"], 1)
            g.memset(keys_t[:, :, :, NKV:KEYS], 0.0).then_inc(s["pads_set"], 1)
            pool.wait_ge(s["pads_set"], 1)
            pool.wait_ge(s["wk_hi_set"], 4)
            g.tensor_tensor(wk_hl[0:DH, HP + 1:H:2, :], wk_raw[DH:P, HP // 2:HP, :],
                            wk_hl[DH:P, HP + 1:H:2, :].bitcast(F32), ALU.subtract).then_inc(s["wk_lo_end_set"], 1)
            pool.wait_ge(s["wk_lo_end_set"], 1)
            norm_front(1, 2)
            pool.wait_ge(s["x0_in"], 16)
            pool.wait_ge(s["x_in"], 16)
            pool.wait_ge(s["bo_in"], 16)
            step(0, True, False)
            with pool.Fori(1, TILES - 1) as t:
                step(t, True, True)
            step(TILES - 1, False, True)
            back_norm(TILES - 1)
            back_rope(TILES - 1, values=False)
            back_y(TILES - 1)
            back_f(TILES - 1)


def kernel(x, ctx_1024, L0_xattn_Wq, L0_xattn_Wkv, L0_xattn_Wout, L0_xattn_bout, L0_attn_Wqkv, L0_attn_bqkv,
           L0_attn_gq, L0_attn_gk, L0_attn_Wout, L0_attn_bout, L0_attn_gout, L0_ffn_packed_weight,
           L0_ffn_weight_scale, L0_ffn_bias):
    import concourse.bacc as _bacc
    from concourse.bass_utils import run_bass_kernel_spmd as _run

    c = np.asarray(ctx_1024).reshape(TILES, TB, NKV, D)
    wkv = np.asarray(L0_xattn_Wkv)
    by_group = c[:, :, :NKV - 1, :].reshape(TILES, TB, M - 1, 2, 2, GQ, D).transpose(0, 4, 2, 5, 1, 3, 6)
    arrays = {
        "x": np.asarray(x).reshape(BATCH * NQ, D),
        "ctx_t": c.reshape(TILES, TB, NKV, KD, P).transpose(0, 4, 3, 1, 2).reshape(TILES, P, KD * TB, NKV),
        "ctx_k": by_group.reshape(TILES, P, TB, 2, D),
        "ctx_9": c[:, :, NKV - 1, :],
        "const": constants(), "rope": rope_table(),
        "wq": L0_xattn_Wq, "wk_t": wkv[:, :INNER].T, "wv": wkv[:, INNER:], "wo": L0_xattn_Wout, "bo": L0_xattn_bout,
        "swqkv_t": np.asarray(L0_attn_Wqkv).T, "sbqkv": L0_attn_bqkv, "sgq": L0_attn_gq, "sgk": L0_attn_gk,
        "swo_t": np.asarray(L0_attn_Wout).T, "sbo": L0_attn_bout, "sgout": L0_attn_gout,
        "packed_t": np.asarray(L0_ffn_packed_weight).reshape(64, D).T,
        "wscale": L0_ffn_weight_scale, "fbias": L0_ffn_bias,
    }
    nc = _bacc.Bacc("TRN2", target_bir_lowering=False, num_devices=1)
    ins, given = {}, {}
    for name, v in arrays.items():
        v = np.ascontiguousarray(v)
        given[f"in_{name}"] = v
        ins[name] = nc.dram_tensor(f"in_{name}", v.shape, mybir.dt.from_np(v.dtype), kind="ExternalInput").ap()
    out = nc.dram_tensor("out", (TILES, P, D), F32, kind="ExternalOutput").ap()
    build(nc, ins, out)
    r = _run(nc, [given], core_ids=[0])
    return r.results[0]["out"].reshape(BATCH, NQ, D)
```
